# Optimizing a Trainium2 kernel written in Bass

```python
import numpy as np
import jax
import jax.numpy as jnp

def _softmax(x, axis=-1):
    return jax.nn.softmax(x, axis=axis)

def _gelu(x):
    return jax.nn.gelu(x, approximate=True)

def _silu(x):
    return jax.nn.silu(x)

def _sigmoid(x):
    return jax.nn.sigmoid(x)

def _layernorm(x, axis=-1, eps=1e-05):
    m = jnp.mean(x, axis=axis, keepdims=True)
    v = jnp.var(x, axis=axis, keepdims=True)
    return (x - m) / jnp.sqrt(v + eps)

def _scatter_add(tgt, idx, src, axis=0):
    return tgt.at[idx].add(src)

def _segment_sum(src, seg, n):
    return jax.ops.segment_sum(src, seg, n)
kernel_name = 'mk_prb_d1_jaxref_r4_00393f'

def setup_inputs(seed: int=0):
    np.random.seed(seed)
    _w = jnp.asarray

    def _L0_attn_setup():
        import jax, jax.numpy as jnp
        import numpy as np
        NUM_HEADS = 16
        EPS = 1e-05
        key = jax.random.key(seed)
        k1, k2, k3 = jax.random.split(key, 3)
        b, n, d = (2, 512, 256)
        x = jax.random.normal(k1, (b, n, d), dtype=jnp.float32)
        wqkv = jax.random.normal(k2, (d, 3 * d), dtype=jnp.float32) * (1.0 / np.sqrt(d))
        wo = jax.random.normal(k3, (d, d), dtype=jnp.float32) * (1.0 / np.sqrt(d))
        return {'x': x, 'wqkv': wqkv, 'wo': wo}
    _L0_attn_in = _L0_attn_setup()

    def _L0_ffn_setup():
        import jax, jax.numpy as jnp
        import numpy as np
        from jax import lax
        H = 256
        E = 8
        E_MLP = E - 4
        TOP_K = 2
        I = 128
        KC = 4
        SHARED_SCALE = 1.0
        key = jax.random.key(seed)
        ks = jax.random.split(key, 8)
        B, S = (4, 1024)
        s_h = 1.0 / np.sqrt(H)
        s_i = 1.0 / np.sqrt(I)
        return {'hidden_states': jax.random.normal(ks[0], (B, S, H), dtype=jnp.float32), 'Wr': jax.random.normal(ks[1], (H, E), dtype=jnp.float32) * s_h, 'router_bias': jnp.zeros((E,), dtype=jnp.float32), 'Wg': jax.random.normal(ks[2], (E_MLP, H, I), dtype=jnp.float32) * s_h, 'Wu': jax.random.normal(ks[3], (E_MLP, H, I), dtype=jnp.float32) * s_h, 'Wd': jax.random.normal(ks[4], (E_MLP, I, H), dtype=jnp.float32) * s_i, 'conv_w': jax.random.normal(ks[5], (KC, 1, H), dtype=jnp.float32) * (1.0 / np.sqrt(KC)), 'conv_b': jnp.zeros((H,), dtype=jnp.float32)}
    _L0_ffn_in = _L0_ffn_setup()
    _d = {'L0_attn_x': _L0_attn_in['x'], 'L0_attn_wqkv': _L0_attn_in['wqkv'], 'L0_attn_wo': _L0_attn_in['wo'], 'L0_ffn_Wr': _L0_ffn_in['Wr'], 'L0_ffn_router_bias': _L0_ffn_in['router_bias'], 'L0_ffn_Wg': _L0_ffn_in['Wg'], 'L0_ffn_Wu': _L0_ffn_in['Wu'], 'L0_ffn_Wd': _L0_ffn_in['Wd'], 'L0_ffn_conv_w': _L0_ffn_in['conv_w'], 'L0_ffn_conv_b': _L0_ffn_in['conv_b']}
    _x0 = _d['L0_attn_x']
    _d['L0_attn_x'] = jax.random.normal(jax.random.fold_in(jax.random.key(seed), 1), (8, 2048, 256), dtype=_x0.dtype)
    del _x0
    return _d

def reference(L0_attn_x, L0_attn_wqkv, L0_attn_wo, L0_ffn_Wr, L0_ffn_router_bias, L0_ffn_Wg, L0_ffn_Wu, L0_ffn_Wd, L0_ffn_conv_w, L0_ffn_conv_b):

    def _L0_attn_ref(x, wqkv, wo):
        import jax, jax.numpy as jnp
        import numpy as np
        NUM_HEADS = 16
        EPS = 1e-05
        b, n, d = x.shape
        h = NUM_HEADS
        hd = d // h
        qkv = x @ wqkv
        q, k, v = jnp.split(qkv, 3, axis=-1)
        q = jax.nn.relu(q)
        k = jax.nn.relu(k)
        split_heads = lambda t: t.reshape(b, n, h, hd).transpose(0, 2, 1, 3)
        q, k, v = (split_heads(q), split_heads(k), split_heads(v))
        kv = jnp.cumsum(k[..., :, None] * v[..., None, :], axis=2)
        num = jnp.einsum('bhnd,bhnde->bhne', q, kv)
        k_sum = jnp.cumsum(k, axis=2)
        den = jnp.einsum('bhnd,bhnd->bhn', q, k_sum)[..., None] + EPS
        y = num / den
        y = y.transpose(0, 2, 1, 3).reshape(b, n, d)
        return y @ wo

    def _L0_ffn_ref(hidden_states, Wr, router_bias, Wg, Wu, Wd, conv_w, conv_b):
        import jax, jax.numpy as jnp
        import numpy as np
        from jax import lax
        H = 256
        E = 8
        E_MLP = E - 4
        TOP_K = 2
        I = 128
        KC = 4
        SHARED_SCALE = 1.0
        B, S, Hd = hidden_states.shape
        T = B * S
        x = hidden_states.reshape(T, Hd)
        scores = jax.nn.sigmoid(x @ Wr)
        _, idx = lax.top_k(scores + router_bias, TOP_K)
        w = jnp.take_along_axis(scores, idx, axis=-1)
        w = w / (jnp.sum(w, axis=-1, keepdims=True) + 1e-09)
        cw = jnp.zeros((T, E), dtype=x.dtype).at[jnp.arange(T)[:, None], idx].add(w)
        g = jnp.einsum('th,ehi->tei', x, Wg)
        u = jnp.einsum('th,ehi->tei', x, Wu)
        hid = jax.nn.silu(g) * u
        mlp_out = jnp.einsum('tei,eih->teh', hid, Wd)
        routed = jnp.einsum('te,teh->th', cw[:, :E_MLP], mlp_out)
        routed = routed + cw[:, E_MLP:E_MLP + 1] * x
        routed = routed + cw[:, E_MLP + 2:E_MLP + 3] * x
        routed = routed + cw[:, E_MLP + 3:E_MLP + 4] * jax.nn.relu(x)
        routed = routed.reshape(B, S, Hd)
        shared = lax.conv_general_dilated(hidden_states, conv_w, window_strides=(1,), padding=[(KC - 1, 0)], dimension_numbers=('NHC', 'HIO', 'NHC'), feature_group_count=Hd) + conv_b
        return routed + SHARED_SCALE * shared
    x = L0_attn_x
    xn = _layernorm(x, axis=-1)
    x = x + _L0_attn_ref(xn, L0_attn_wqkv, L0_attn_wo) + _L0_ffn_ref(xn, L0_ffn_Wr, L0_ffn_router_bias, L0_ffn_Wg, L0_ffn_Wu, L0_ffn_Wd, L0_ffn_conv_w, L0_ffn_conv_b)
    return x

_drawn_inputs = setup_inputs


def setup_inputs(seed=0):
    import zlib

    import numpy as np

    out = dict(_drawn_inputs(seed))
    spreads = {'L0_ffn_router_bias': (0.0, 0.1), 'L0_ffn_conv_b': (0.0, 0.1)}
    factors = {}
    for name, (base, spread) in spreads.items():
        noise = np.random.default_rng([zlib.crc32(name.encode()), seed]).standard_normal(out[name].shape)
        drawn = base * np.exp(spread * noise) if base else spread * noise
        out[name] = jnp.asarray(drawn.astype(out[name].dtype))
    for name, factor in factors.items():
        out[name] = (out[name] * factor).astype(out[name].dtype)
    return out
```

```python
from contextlib import ExitStack

import concourse.bass as bass
from concourse import mybir

F32 = mybir.dt.float32
F32R = mybir.dt.float32r
U32 = mybir.dt.uint32
ALU = mybir.AluOpType
ACT = mybir.ActivationFunctionType
AX = mybir.AxisListType

P = 128


def layer_kernel(nc, x, wqkv, wo, w_router, router_bias, w_gate, w_up, w_down, conv_w, conv_b,
                 ident, causal, same_head, parity, expert_rows, iota, out):
    n_seq, seq_len, D = x.shape
    E, _, I = w_gate.shape
    NR = w_router.shape[1]
    HD = 16
    C = D // P
    T = 4
    BT = T * P
    BPS = seq_len // BT
    TAPS = conv_w.shape[2]
    HALO = TAPS - 1
    EPS_LN, EPS_DEN, EPS_W = 1e-5, 1e-5, 1e-9
    VW = D + NR
    PAIRS = D // (2 * HD)
    PPG = PAIRS // C
    assert I == P and E == T and D == C * P and PPG == 4 and BPS == 4

    x_v = x.rearrange("s (b t p) c -> (s b) p t c", p=P, t=T)
    out_v = out.rearrange("s (b t p) c -> (s b) p t c", p=P, t=T)

    with ExitStack() as ctx:
        def sb(name, shape, dt=F32):
            return ctx.enter_context(nc.sbuf_tensor(name, shape, dt))

        def bank(name):
            return ctx.enter_context(nc.psum_tensor(name, [P, BT], F32))

        def sem(name):
            return ctx.enter_context(nc.semaphore(name))

        wqk_h, wqk_l = sb("wqk_h", [P, C, 2 * D], F32R), sb("wqk_l", [P, C, 2 * D], F32R)
        wvr_h, wvr_l = sb("wvr_h", [P, C, VW], F32R), sb("wvr_l", [P, C, VW], F32R)
        wgu_h, wgu_l = sb("wgu_h", [P, 2, E, C, I], F32R), sb("wgu_l", [P, 2, E, C, I], F32R)
        wd_h, wd_l = sb("wd_h", [P, E, D], F32R), sb("wd_l", [P, E, D], F32R)
        wo_h, wo_l = sb("wo_h", [P, C, D], F32R), sb("wo_l", [P, C, D], F32R)
        conv_ws = sb("conv_ws", [P, C, TAPS])
        conv_bs = sb("conv_bs", [P, C])
        bias_s = sb("bias_s", [P, NR])
        ident_s = sb("ident_s", [P, P])
        causal_s = sb("causal_s", [P, P])
        same_head_s = sb("same_head_s", [P, P])
        parity_s = sb("parity_s", [P, 2])
        sel = sb("sel", [2 * E, E, P], F32R)
        iota_s = sb("iota_s", [P, T, NR])
        zeros = sb("zeros", [P, BT])
        half = sb("half", [P, T])
        spare = sb("spare", [P, 1])
        x_t = sb("x_t", [P, 2, T, D])
        xn = sb("xn", [P, T, D])
        stats = sb("stats", [P, T, 6])
        mv = sb("mv", [P, T, 2])
        negm = sb("negm", [P, T])
        vare = sb("vare", [P, T])
        rstd = sb("rstd", [P, T])
        xT = sb("xT", [P, C, HALO + BT])
        xh, xl = sb("xh", [P, C, BT], F32R), sb("xl", [P, C, BT], F32R)
        kT = sb("kT", [P, C, BT])
        kh, kl = sb("kh", [P, C, BT], F32R), sb("kl", [P, C, BT], F32R)
        qT = sb("qT", [P, C, BT])
        qh, ql = sb("qh", [P, C, 2, BT], F32R), sb("ql", [P, C, 2, BT], F32R)
        ksum = sb("ksum", [P, 2, C, BT])
        qks = sb("qks", [P, C, BT])
        den = sb("den", [P, C, BT])
        rden = sb("rden", [P, C, P])
        vp = sb("vp", [P, T, PAIRS, 3, HD])
        score = sb("score", [P, T, NR])
        scoreb = sb("scoreb", [P, T, NR])
        top = sb("top", [P, T, 8])
        topi = sb("topi", [P, T, 8], U32)
        hot = sb("hot", [P, 2, T, NR])
        picked = sb("picked", [P, T, NR])
        wsum = sb("wsum", [P, 3, T])
        cw = sb("cw", [P, T, NR])
        c46 = sb("c46", [P, T, 1])
        cws = sb("cws", [P, T, 2 * E], F32R)
        cwT = sb("cwT", [2 * E, BT], F32R)
        sm = sb("sm", [P, 2 * PAIRS, P])
        ktok = sb("ktok", [P, D])
        state = sb("state", [P, D])
        state_bd = sb("state_bd", [P, D])
        yT = sb("yT", [P, C, BT])
        yh, yl = sb("yh", [P, C, BT], F32R), sb("yl", [P, C, BT], F32R)
        sg = sb("sg", [P, 2, BT])
        gu = sb("gu", [P, BT])
        hid = sb("hid", [P, E, BT])
        hh, hl = sb("hh", [P, E, BT], F32R), sb("hl", [P, E, BT], F32R)
        cT = sb("cT", [P, 2, C, BT])

        st_qkv = hid[:, :, :].rearrange("p e n -> p (e n)")[:, 0:C * 3 * D].rearrange("p (c n) -> p c n", c=C)
        st_g = sm[:, 0:8, :].rearrange("p h n -> p (h n)").rearrange("p (e c i) -> p e c i", e=E, c=C)
        st_u = sm[:, 8:16, :].rearrange("p h n -> p (h n)").rearrange("p (e c i) -> p e c i", e=E, c=C)
        st_d = qT[:, :, :].rearrange("p c n -> p (c n)").rearrange("p (e n) -> p e n", e=E)
        st_o = ksum[:, 0, 0, :].rearrange("p (c n) -> p c n", c=C)
        st_r = ksum[:, 0, 1, 0:C * NR].rearrange("p (c n) -> p c n", c=C)
        st_sel = ksum[0:2 * E, 1, 0, 0:E * P].rearrange("p (e n) -> p e n", e=E)

        R = [bank(f"ring{k}") for k in range(3)]
        SB = [bank(f"scores{k}") for k in range(2)]
        NUM, TR, ST = bank("num"), bank("turned"), bank("state_add")

        w_in = sem("w_in")
        w_split = sem("w_split")
        w_hi = sem("w_hi")
        set_up = sem("set_up")
        x_in = [sem("x_in0"), sem("x_in1")]
        stored = [sem("stored0"), sem("stored1")]
        s_stats = sem("s_stats")
        s_rstd = sem("s_rstd")
        s_xn = sem("s_xn")
        s_xtr = sem("s_xtr")
        s_xT = sem("s_xT")
        s_halo = sem("s_halo")
        s_xh = sem("s_xh")
        s_xl = sem("s_xl")
        s_kp = sem("s_kp")
        s_kT = sem("s_kT")
        s_kh = sem("s_kh")
        s_kl = sem("s_kl")
        s_qp = sem("s_qp")
        s_qT = sem("s_qT")
        s_qh = sem("s_qh")
        s_ql = sem("s_ql")
        s_vp = sem("s_vp")
        s_v = sem("s_v")
        s_sig = sem("s_sig")
        s_cw = sem("s_cw")
        s_cws = sem("s_cws")
        s_cwtr = sem("s_cwtr")
        s_cwT = sem("s_cwT")
        s_qks = sem("s_qks")
        s_denp = sem("s_denp")
        s_den = sem("s_den")
        s_gp = sem("s_gp")
        s_sg = sem("s_sg")
        s_up = sem("s_up")
        s_gu = sem("s_gu")
        s_cwp = sem("s_cwp")
        s_hid = sem("s_hid")
        s_hh = sem("s_hh")
        s_hl = sem("s_hl")
        s_s = sem("s_s")
        s_sm = sem("s_sm")
        s_ktr = sem("s_ktr")
        s_ktok = sem("s_ktok")
        s_num = sem("s_num")
        s_y = sem("s_y")
        s_yh = sem("s_yh")
        s_yl = sem("s_yl")
        s_st = sem("s_st")
        s_state = sem("s_state")
        s_bd = sem("s_bd")
        s_conv = sem("s_conv")
        s_base1 = sem("s_base1")
        s_relu7 = sem("s_relu7")
        s_base2 = sem("s_base2")
        s_op = sem("s_op")
        s_out = sem("s_out")
        s_own = sem("s_own")

        N_BATCH = n_seq * BPS
        LOADS = [0]

        def rounds(engine, body):
            with engine.Fori(0, n_seq - 1) as s:
                for j in range(BPS):
                    body(s, j, BPS)
            for j in range(BPS):
                body(n_seq - 1, j, BPS - 1 - j)

        def at(s, j, per, k):
            return s * (BPS * per) + (j * per + k)

        SPLITS = [("qk", wqk_h[:, c, :], wqk_l[:, c, :], st_qkv[:, c, 0:2 * D]) for c in range(C)]
        SPLITS += [("v", wvr_h[:, c, 0:D], wvr_l[:, c, 0:D], st_qkv[:, c, 2 * D:3 * D]) for c in range(C)]
        SPLITS += [("router", wvr_h[:, :, D:VW], wvr_l[:, :, D:VW], st_r)]
        SPLITS += [("gate", wgu_h[:, 0], wgu_l[:, 0], st_g), ("up", wgu_h[:, 1], wgu_l[:, 1], st_u)]
        SPLITS += [("down", wd_h[:, :, :], wd_l[:, :, :], st_d), ("out", wo_h[:, :, :], wo_l[:, :, :], st_o)]
        N_SPLITS = len(SPLITS)
        OWN_SETUP = 2 + (TAPS - 1)
        OWN_BATCH = 1 + 11 + T + 2 + (TAPS - 1)

        def settled(engine):
            engine.wait_ge(set_up, 4)

        block = ctx.enter_context(nc.Block())

        @block.sync
        def _(sp):
            def load(dst, src):
                sp.dma_start(dst, src).then_inc(w_in, 16)
                LOADS[0] += 1
            sp.dma_start(x_t[:, 0], x_v[0]).then_inc(x_in[0], 16)
            for c in range(C):
                load(st_qkv[:, c, :], wqkv[c * P:(c + 1) * P, :])
                load(st_o[:, c, :], wo[c * P:(c + 1) * P, :])
                load(st_r[:, c, :], w_router[c * P:(c + 1) * P, :])
            load(conv_ws[:, :, :], conv_w)
            load(conv_bs[:, :], conv_b)
            for src, dst in ((w_gate, st_g), (w_up, st_u)):
                for c in range(C):
                    load(dst[:, :, c, :], src[:, c * P:(c + 1) * P, :].rearrange("e p i -> p e i"))
            load(st_d, w_down.rearrange("e p n -> p e n"))
            load(bias_s[:, :], router_bias)
            load(ident_s[:, :], ident)
            load(causal_s[:, :], causal)
            load(same_head_s[:, :], same_head)
            load(parity_s[:, :], parity)
            load(st_sel, expert_rows)
            load(iota_s[:, :, :], iota)
            sp.dma_start(x_t[:, 1], x_v[1]).then_inc(x_in[1], 16)

            def batch(s, j, left):
                b = s * BPS + j
                sp.wait_ge(s_out, at(s, j, T, 2 * T))
                sp.dma_start(out_v[b], x_t[:, j % 2]).then_inc(stored[j % 2], 16)
                if left < 2:
                    return
                sp.wait_ge(stored[j % 2], s * (BPS // 2 * 16) + (j // 2 + 1) * 16)
                sp.dma_start(x_t[:, j % 2], x_v[b + 2]).then_inc(x_in[j % 2], 16)

            rounds(sp, batch)
            for p in range(2):
                sp.wait_ge(stored[p], N_BATCH // 2 * 16)

        N_LOADS = LOADS[0]

        @block.tensor
        def _(pe):
            mm = nc.tensor.matmul

            def turn_xn(s, j, k):
                pe.wait_ge(s_xn, at(s, j, 1, k + 1))
                for c in range(C):
                    if c > 0:
                        pe.wait_ge(s_xT, at(s, j, C, k * C + c))
                    for t in range(T):
                        ins = nc.tensor.transpose(TR[:, t * P:(t + 1) * P], xn[:, t, c * P:(c + 1) * P], ident_s[:, :])
                    ins.then_inc(s_xtr, 1)

            def product(dst, pairs, first=True, final=True):
                passes = [q for lh, ll, rh, rl in pairs for q in ((lh, rl), (lh, rh), (ll, rh))]
                for n, (lhs, rhs) in enumerate(passes):
                    ins = mm(dst, lhs, rhs, start=first and n == 0, stop=final and n == len(passes) - 1,
                             skip_group_check=not first)
                return ins

            def batch(s, j, left):
                last = left == 0
                pe.wait_ge(s_xh, at(s, j, C, C))
                pe.wait_ge(s_xl, at(s, j, C, C))

                def project(dst, h, l, col):
                    return product(dst, [(h[:, c, col:col + P], l[:, c, col:col + P], xh[:, c, :], xl[:, c, :])
                                         for c in range(C)])

                for t in range(T):
                    if t < 3:
                        pe.wait_ge(s_out, at(s, j, T, 2 + t))
                    else:
                        pe.wait_ge(s_sig, at(s, j, T, 1))
                    ts = slice(t * P, (t + 1) * P)
                    product(R[t % 3][:, 0:VW], [(xh[:, c, ts], xl[:, c, ts], wvr_h[:, c, :], wvr_l[:, c, :])
                                                for c in range(C)]).then_inc(s_vp, 1)
                for g in range(C):
                    pe.wait_ge(s_sig, at(s, j, T, 2 + g))
                    project(R[1 + g][:, :], wqk_h, wqk_l, D + g * P).then_inc(s_kp, 1)
                pe.wait_ge(s_sig, at(s, j, T, 4))
                project(R[0][:, :], wqk_h, wqk_l, 0).then_inc(s_qp, 1)
                pe.wait_ge(s_kT, at(s, j, C, 1))
                project(R[1][:, :], wqk_h, wqk_l, P).then_inc(s_qp, 1)

                def score_bank(t, f):
                    if f >= 2:
                        pe.wait_ge(s_sm, at(s, j, 16, 4 * t + f - 1))
                    ts = slice(t * P, (t + 1) * P)
                    rows = slice(32 * f, 32 * f + 32)
                    for g in range(C):
                        dst = SB[f % 2][:, g * 2 * P:(g + 1) * 2 * P]
                        ins = product(dst, [(kh[rows, g, ts], kl[rows, g, ts], qh[rows, g, :, ts], ql[rows, g, :, ts])])
                    ins.then_inc(s_s, 1)

                def gate(t, u):
                    product(R[u][:, :], [((wgu_h[:, u, t, c, :]), wgu_l[:, u, t, c, :], xh[:, c, :], xl[:, c, :])
                                         for c in range(C)]).then_inc(s_up if u else s_gp, 1)

                def denominator(g):
                    pe.wait_ge(s_qks, at(s, j, C, g + 1))
                    if g == 0:
                        pe.wait_ge(s_kT, at(s, j, C, 2))
                    else:
                        pe.wait_ge(s_sg, at(s, j, T, 1))
                    mm(R[2 - 2 * g][:, :], same_head_s[:, :], qks[:, g, :], start=True, stop=True).then_inc(s_denp, 1)

                def numerators(t):
                    ts = slice(t * P, (t + 1) * P)
                    if t:
                        pe.wait_ge(s_y, at(s, j, T, t))
                    first_tile = j == 0 and t == 0
                    if not first_tile:
                        pe.wait_ge(s_bd, at(s, j, T, t))
                    for g in range(C):
                        gs = slice(g * P, (g + 1) * P)
                        pe.wait_ge(s_sm, at(s, j, 16, 4 * t + 4))
                        if not first_tile:
                            mm(NUM[:, gs], state_bd[:, gs], qT[:, g, ts], start=True, stop=False)
                        for par in range(2):
                            for m in range(PPG):
                                pair = g * PPG + m
                                window = vp[:, t, pair, par:par + 2, :].rearrange("p a d -> p (a d)")
                                ins = mm(NUM[32 * m:32 * m + 32, gs], window, sm[:, 2 * pair + par, :],
                                         start=first_tile and par == 0, stop=par == 1)
                    ins.then_inc(s_num, 1)
                    pe.wait_ge(s_ktok, at(s, j, T, t + 1))
                    if t:
                        pe.wait_ge(s_state, at(s, j, T, t))
                    for g in range(C):
                        gs = slice(g * P, (g + 1) * P)
                        ins = mm(ST[:, gs], ktok[:, gs], vp[:, t, g * PPG:(g + 1) * PPG, 0:3:2, :],
                                 start=True, stop=True)
                    ins.then_inc(s_st, 1)

                pe.wait_ge(s_qT, at(s, j, C, 1))
                gate(0, 0)
                pe.wait_ge(s_qT, at(s, j, C, 2))
                gate(0, 1)
                pe.wait_ge(s_cws, at(s, j, 1, 1))
                pe.wait_ge(s_xT, at(s, j, C, C))
                for t in range(T):
                    ins = nc.tensor.transpose(TR[0:2 * E, t * P:(t + 1) * P], cws[:, t, :].bitcast(F32), ident_s[:, :])
                ins.then_inc(s_cwtr, 1)
                denominator(0)
                pe.wait_ge(s_kl, at(s, j, C, C))
                pe.wait_ge(s_ql, at(s, j, C, C))
                for t in range(T):
                    ts = slice(t * P, (t + 1) * P)
                    score_bank(t, 0)
                    score_bank(t, 1)
                    if t == 0:
                        denominator(1)
                    else:
                        pe.wait_ge(s_gu, at(s, j, T, t))
                        gate(t, 1)
                    score_bank(t, 2)
                    score_bank(t, 3)
                    if t == 0:
                        pe.wait_ge(s_cwT, at(s, j, 1, 1))
                    else:
                        pe.wait_ge(s_ktok, at(s, j, T, t))
                    for g in range(C):
                        ins = nc.tensor.transpose(TR[:, g * P:(g + 1) * P], kT[:, g, ts], ident_s[:, :])
                    ins.then_inc(s_ktr, 1)
                    if t == 0:
                        pe.wait_ge(s_den, at(s, j, C, 1))
                    else:
                        pe.wait_ge(s_hid, at(s, j, T, t))
                    mm(R[2][:, :], sel[:, t, :], cwT[:, :], start=True, stop=True).then_inc(s_cwp, 1)
                    if t < T - 1:
                        if t == 0:
                            pe.wait_ge(s_den, at(s, j, C, 2))
                        else:
                            pe.wait_ge(s_sg, at(s, j, T, t + 1))
                        gate(t + 1, 0)
                    elif not last:
                        pe.wait_ge(s_ktok, at(s, j, T, T))
                        turn_xn(s, j, 1)
                    numerators(t)

                for t in range(T):
                    ts = slice(t * P, (t + 1) * P)
                    bank_o = R[(t + 2) % 3]
                    if t == 0:
                        pe.wait_ge(s_hid, at(s, j, T, T))
                        pe.wait_ge(s_conv, at(s, j, 1, 1))
                    elif t == 1:
                        pe.wait_ge(s_sg, at(s, j, T, T))
                    elif t == 2:
                        pe.wait_ge(s_gu, at(s, j, T, T))
                    else:
                        pe.wait_ge(s_out, at(s, j, T, T + 1))
                    for c in range(C):
                        mm(bank_o[:, c * P:(c + 1) * P], cT[:, j % 2, c, ts], ident_s[:, :], is_transpose=True,
                           start=c == 0, stop=False, skip_group_check=True)
                    if t == 0:
                        pe.wait_ge(s_hh, at(s, j, T, T))
                        pe.wait_ge(s_hl, at(s, j, T, T))
                    product(bank_o[:, 0:D], [(hh[:, e, ts], hl[:, e, ts], wd_h[:, e, :], wd_l[:, e, :])
                                             for e in range(E)], first=False, final=False)
                    if t == 0:
                        pe.wait_ge(s_yh, at(s, j, T, T))
                        pe.wait_ge(s_yl, at(s, j, T, T))
                    product(bank_o[:, 0:D], [(yh[:, c, ts], yl[:, c, ts], wo_h[:, c, :], wo_l[:, c, :])
                                             for c in range(C)], first=False).then_inc(s_op, 1)

            pe.wait_ge(w_in, 16 * N_LOADS)
            turn_xn(0, 0, 0)
            pe.wait_ge(w_split, N_SPLITS)
            pe.wait_ge(set_up, 4)
            rounds(pe, batch)

        @block.scalar
        def _(act):
            copy = lambda o, i: nc.scalar.activation(o, i, ACT.Copy)
            act.wait_ge(w_in, 16 * N_LOADS)
            for _, hi, _, src in SPLITS:
                copy(hi, src).then_inc(w_hi, 1)
            copy(sel[:, :, :], st_sel).then_inc(set_up, 1)

            def fill_xT(s, j, k):
                if k:
                    act.wait_ge(s_conv, at(s, j, 1, 1))
                if k and j < BPS - 1:
                    act.activation(xT[:, :, 0:HALO], xT[:, :, BT:BT + HALO], ACT.Copy).then_inc(s_halo, 1)
                else:
                    act.activation(xT[:, :, 0:HALO], zeros[:, 0:C * HALO].rearrange("p (c h) -> p c h", c=C),
                                   ACT.Copy).then_inc(s_halo, 1)
                act.wait_ge(s_halo, at(s, j, 1, k + 1))
                for c in range(C):
                    act.wait_ge(s_xtr, at(s, j, C, k * C + c + 1))
                    copy(xT[:, c, HALO:HALO + BT], TR[:, :]).then_inc(s_xT, 1)

            def batch(s, j, left):
                last = left == 0
                kb, qb = [R[1], R[2]], [R[0], R[1]]
                for t in range(T):
                    act.wait_ge(s_vp, at(s, j, T, t + 1))
                    copy(vp[:, t, :, 0:3:2, :],
                         R[t % 3][:, 0:D].rearrange("p (a b d) -> p a b d", a=PAIRS, b=2)).then_inc(s_v, 1)
                    act.activation(score[:, t, :], R[t % 3][:, D:VW], ACT.Sigmoid).then_inc(s_sig, 1)
                for g in range(C):
                    act.wait_ge(s_kp, at(s, j, C, g + 1))
                    act.activation(kT[:, g, :], kb[g][:, :], ACT.Relu).then_inc(s_kT, 1)
                    act.wait_ge(s_kT, at(s, j, C, g + 1))
                    copy(kh[:, g, :], kT[:, g, :]).then_inc(s_kh, 1)
                for g in range(C):
                    act.wait_ge(s_qp, at(s, j, C, g + 1))
                    act.activation(qT[:, g, :], qb[g][:, :], ACT.Relu).then_inc(s_qT, 1)
                    act.wait_ge(s_qT, at(s, j, C, g + 1))
                    for par in range(2):
                        ins = act.activation(qh[:, g, par, :], qT[:, g, :], ACT.Copy, scale=parity_s[:, par:par + 1])
                    ins.then_inc(s_qh, 1)
                for t in range(T):
                    act.wait_ge(s_gp, at(s, j, T, t + 1))
                    act.activation(sg[:, t % 2, :], R[0][:, :], ACT.Silu).then_inc(s_sg, 1)
                    if t == 0:
                        act.wait_ge(s_cwtr, at(s, j, 1, 1))
                        copy(cwT[:, :], TR[0:2 * E, :]).then_inc(s_cwT, 1)
                        for g in range(C):
                            act.wait_ge(s_denp, at(s, j, C, g + 1))
                            act.activation(den[:, g, :], R[2 - 2 * g][:, :], ACT.Copy, bias=EPS_DEN).then_inc(s_den, 1)
                    act.wait_ge(s_ktr, at(s, j, T, t + 1))
                    copy(ktok[:, :], TR[:, 0:D]).then_inc(s_ktok, 1)
                    act.wait_ge(s_hid, at(s, j, T, t + 1))
                    copy(hh[:, t, :], hid[:, t, :]).then_inc(s_hh, 1)
                    if t == 1:
                        act.wait_ge(s_base1, at(s, j, 1, 1))
                        for tt in range(T):
                            ins = act.activation(xn[:, tt, :], xn[:, tt, :], ACT.Relu, scale=cw[:, tt, NR - 1:NR])
                        ins.then_inc(s_relu7, 1)
                    if t == T - 1 and not last:
                        fill_xT(s, j, 1)
                    act.wait_ge(s_y, at(s, j, T, t + 1))
                    ts = slice(t * P, (t + 1) * P)
                    copy(yh[:, :, ts], yT[:, :, ts]).then_inc(s_yh, 1)

            act.wait_ge(set_up, 4)
            fill_xT(0, 0, 0)
            rounds(act, batch)

        @block.gpsimd
        def _(pool):
            pool.memset(zeros[:, :], 0.0).then_inc(set_up, 1)
            pool.memset(half[:, :], -0.5).then_inc(set_up, 1)
            pool.memset(vp[:, :, :, :, :], 0.0).then_inc(set_up, 1)

            def normalise(s, j, k):
                pool.wait_ge(s_stats, at(s, j, 1, k + 1))
                pool.tensor_tensor(rstd[:, :], vare[:, :], half[:, :], ALU.pow).then_inc(s_rstd, 1)
                settled(pool)
                pool.wait_ge(s_rstd, at(s, j, 1, k + 1))
                for t in range(T):
                    ins = pool.tensor_scalar(xn[:, t, :], x_t[:, (j + k) % 2, t, :], negm[:, t:t + 1],
                                             rstd[:, t:t + 1], ALU.add, ALU.mult)
                ins.then_inc(s_xn, 1)

            def low_x(s, j, k):
                for c in range(C):
                    pool.wait_ge(s_xh, at(s, j, C, k * C + c + 1))
                    pool.tensor_tensor(xl[:, c, :], xT[:, c, HALO:HALO + BT], xh[:, c, :].bitcast(F32),
                                       ALU.subtract).then_inc(s_xl, 1)

            def batch(s, j, left):
                last = left == 0
                for g in range(C):
                    pool.wait_ge(s_kh, at(s, j, C, g + 1))
                    pool.tensor_tensor(kl[:, g, :], kT[:, g, :], kh[:, g, :].bitcast(F32),
                                       ALU.subtract).then_inc(s_kl, 1)
                for t in range(T):
                    ts = slice(t * P, (t + 1) * P)
                    pool.wait_ge(s_hh, at(s, j, T, t + 1))
                    pool.tensor_tensor(hl[:, t, :], hid[:, t, :], hh[:, t, :].bitcast(F32),
                                       ALU.subtract).then_inc(s_hl, 1)
                    pool.wait_ge(s_state, at(s, j, T, t + 1))
                    for g in range(C):
                        gs = slice(g * P, (g + 1) * P)
                        ins = pool.tensor_tensor(state_bd[:, gs], state[:, gs], same_head_s[:, :], ALU.mult)
                    ins.then_inc(s_bd, 1)
                    pool.wait_ge(s_yh, at(s, j, T, t + 1))
                    pool.tensor_tensor(yl[:, :, ts], yT[:, :, ts], yh[:, :, ts].bitcast(F32),
                                       ALU.subtract).then_inc(s_yl, 1)
                    if t == 1:
                        pool.wait_ge(s_relu7, at(s, j, 1, 1))
                        xb = x_t[:, j % 2, :, :]
                        pool.tensor_tensor(xb, xb, xn[:, :, :], ALU.add).then_inc(s_base2, 1)
                    if t == 1 and not last:
                        pool.wait_ge(s_base2, at(s, j, 1, 1))
                        normalise(s, j, 1)
                if not last:
                    low_x(s, j, 1)

            pool.wait_ge(set_up, 4)
            normalise(0, 0, 0)
            low_x(0, 0, 0)
            rounds(pool, batch)

        @block.vector
        def _(dve):
            def statistics(s, j, k):
                p = (j + k) % 2
                dve.wait_ge(x_in[p], s * (BPS // 2 * 16) + ((j + k) // 2 + 1) * 16)
                for t in range(T):
                    ins = dve.bn_stats(stats[:, t, :], x_t[:, p, t, :])
                own(ins, s, j, apart=True)
                for t in range(T):
                    ins = dve.bn_aggr(mv[:, t, :], stats[:, t, :])
                own(ins, s, j)
                dve.tensor_scalar(negm[:, :], mv[:, :, 0], -1.0, None, ALU.mult)
                dve.tensor_scalar(vare[:, :], mv[:, :, 1], EPS_LN, None, ALU.add).then_inc(s_stats, 1)

            count = {"setup": 0, "batch": 0, "in_batch": False}

            def own(ins, s, j, apart=False):
                ins.then_inc(s_own, 1)
                if not count["in_batch"]:
                    count["setup"] += 1
                    dve.wait_ge(s_own, count["setup"])
                    return
                count["batch"] += 1
                dve.wait_ge(s_own, s * (BPS * OWN_BATCH) + (j * OWN_BATCH + count["batch"] + OWN_SETUP))
                if apart:
                    dve.memset(spare[:, :], 0.0)

            def high_x(s, j, k):
                for c in range(C):
                    dve.wait_ge(s_xT, at(s, j, C, k * C + c + 1))
                    dve.tensor_copy(xh[:, c, :], xT[:, c, HALO:HALO + BT]).then_inc(s_xh, 1)

            def router(s, j):
                dve.wait_ge(s_sig, at(s, j, T, T))
                bias_b = bias_s[:, :].unsqueeze(1).to_broadcast([P, T, NR])
                own(dve.tensor_tensor(scoreb[:, :, :], score[:, :, :], bias_b, ALU.add), s, j, apart=True)
                for t in range(T):
                    ins = dve.max(top[:, t, :], scoreb[:, t, :])
                own(ins, s, j, apart=True)
                for t in range(T):
                    ins = dve.max_index(topi[:, t, :], top[:, t, :], scoreb[:, t, :])
                own(ins, s, j)
                for n in range(2):
                    ins = dve.tensor_tensor(hot[:, n, :, :], iota_s[:, :, :],
                                            topi[:, :, n:n + 1].to_broadcast([P, T, NR]), ALU.is_equal)
                own(ins, s, j)
                own(dve.tensor_tensor(hot[:, 0, :, :], hot[:, 0, :, :], hot[:, 1, :, :], ALU.add), s, j)
                own(dve.tensor_tensor(picked[:, :, :], hot[:, 0, :, :], score[:, :, :], ALU.mult), s, j)
                own(dve.tensor_reduce(wsum[:, 0, :], picked[:, :, :], AX.X, ALU.add), s, j)
                own(dve.tensor_scalar(wsum[:, 1, :], wsum[:, 0, :], EPS_W, None, ALU.add), s, j)
                own(dve.reciprocal(wsum[:, 2, :], wsum[:, 1, :]), s, j)
                own(dve.tensor_tensor(cw[:, :, :], picked[:, :, :],
                                      wsum[:, 2, :].unsqueeze(2).to_broadcast([P, T, NR]), ALU.mult), s, j)
                own(dve.tensor_copy(cws[:, :, 0:E], cw[:, :, 0:E]), s, j)
                dve.tensor_tensor(cws[:, :, E:2 * E], cw[:, :, 0:E], cws[:, :, 0:E].bitcast(F32),
                                  ALU.subtract).then_inc(s_cws, 1)
                dve.tensor_tensor(c46[:, :, :], cw[:, :, E:E + 1], cw[:, :, E + 2:E + 3], ALU.add).then_inc(s_cw, 1)

            def conv_tap(s, j, k, tap):
                for c in range(C):
                    src, dst = xT[:, c, tap:tap + BT], cT[:, (j + k) % 2, c, :]
                    if tap == 0:
                        ins = dve.tensor_scalar(dst, src, conv_ws[:, c, 0:1], conv_bs[:, c:c + 1], ALU.mult, ALU.add)
                    else:
                        ins = dve.scalar_tensor_tensor(out=dst, in0=src, scalar=conv_ws[:, c, tap:tap + 1],
                                                       in1=dst, op0=ALU.mult, op1=ALU.add)
                if tap < TAPS - 1:
                    own(ins, s, j)
                else:
                    ins.then_inc(s_conv, 1)

            def batch(s, j, left):
                last = left == 0
                count["batch"], count["in_batch"] = 0, True
                router(s, j)
                for g in range(C):
                    dve.wait_ge(s_kT, at(s, j, C, g + 1))
                    before = ksum[:, (j + 1) % 2, g, BT - 1:BT] if j else 0.0
                    ins = dve.tensor_tensor_scan(ksum[:, j % 2, g, :], kT[:, g, :], zeros[:, :], before,
                                                 ALU.add, ALU.add)
                own(ins, s, j)
                for g in range(C):
                    dve.wait_ge(s_qT, at(s, j, C, g + 1))
                    dve.tensor_tensor(qks[:, g, :], qT[:, g, :], ksum[:, j % 2, g, :], ALU.mult).then_inc(s_qks, 1)
                    dve.wait_ge(s_qh, at(s, j, C, g + 1))
                    for par in range(2):
                        ins = dve.scalar_tensor_tensor(out=ql[:, g, par, :], in0=qT[:, g, :],
                                                       scalar=parity_s[:, par:par + 1],
                                                       in1=qh[:, g, par, :].bitcast(F32),
                                                       op0=ALU.mult, op1=ALU.subtract)
                    ins.then_inc(s_ql, 1)

                def mask(t, f):
                    dve.wait_ge(s_s, at(s, j, 16, 4 * t + f + 1))
                    heads = sm[:, :, :].rearrange("p (g m a) n -> p g m (a n)", g=C, a=2)[:, :, f, :]
                    dve.tensor_tensor(heads.rearrange("p g (a n) -> p g a n", a=2),
                                      SB[f % 2][:, :].rearrange("p (g a n) -> p g a n", g=C, a=2),
                                      causal_s[:, :].unsqueeze(1).unsqueeze(1).to_broadcast([P, C, 2, P]),
                                      ALU.mult).then_inc(s_sm, 1)

                def gate_up(t):
                    dve.wait_ge(s_sg, at(s, j, T, t + 1))
                    dve.wait_ge(s_up, at(s, j, T, t + 1))
                    dve.tensor_tensor(gu[:, :], R[1][:, :], sg[:, t % 2, :], ALU.mult).then_inc(s_gu, 1)

                for t in range(T):
                    ts = slice(t * P, (t + 1) * P)
                    if t == 0:
                        gate_up(t)
                    mask(t, 0)
                    mask(t, 1)
                    if t > 0:
                        gate_up(t)
                    mask(t, 2)
                    mask(t, 3)
                    dve.wait_ge(s_gu, at(s, j, T, t + 1))
                    dve.wait_ge(s_cwp, at(s, j, T, t + 1))
                    dve.tensor_tensor(hid[:, t, :], R[2][:, :], gu[:, :], ALU.mult).then_inc(s_hid, 1)
                    dve.wait_ge(s_den, at(s, j, C, C))
                    own(dve.reciprocal(rden[:, :, :], den[:, :, ts]), s, j)
                    if t == 0:
                        dve.wait_ge(s_cw, at(s, j, 1, 1))
                        for tt in range(T):
                            xb = x_t[:, j % 2, tt, :]
                            ins = dve.scalar_tensor_tensor(out=xb, in0=xn[:, tt, :], scalar=c46[:, tt, :],
                                                           in1=xb, op0=ALU.mult, op1=ALU.add)
                        ins.then_inc(s_base1, 1)
                    if t == 1 and not last:
                        statistics(s, j, 1)
                    dve.wait_ge(s_num, at(s, j, T, t + 1))
                    dve.tensor_tensor(yT[:, :, ts], NUM[:, 0:D].rearrange("p (g n) -> p g n", g=C), rden[:, :, :],
                                      ALU.mult).then_inc(s_y, 1)
                    dve.wait_ge(s_st, at(s, j, T, t + 1))
                    if j == 0 and t == 0:
                        dve.tensor_copy(state[:, :], ST[:, 0:D]).then_inc(s_state, 1)
                    else:
                        dve.tensor_tensor(state[:, :], ST[:, 0:D], state[:, :], ALU.add).then_inc(s_state, 1)
                if not last:
                    high_x(s, j, 1)
                dve.wait_ge(s_base2, at(s, j, 1, 1))
                for t in range(T):
                    dve.wait_ge(s_op, at(s, j, T, t + 1))
                    xb = x_t[:, j % 2, t, :]
                    dve.tensor_tensor(xb, R[(t + 2) % 3][:, 0:D], xb, ALU.add).then_inc(s_out, 1)
                    if not last:
                        conv_tap(s, j, 1, t)
                if not last:
                    assert count["batch"] == OWN_BATCH, count

            dve.wait_ge(w_in, 16 * N_LOADS)
            for n, (_, hi, lo, src) in enumerate(SPLITS):
                dve.wait_ge(w_hi, n + 1)
                dve.tensor_tensor(lo, src, hi.bitcast(F32), ALU.subtract).then_inc(w_split, 1)
            dve.memset(gu[:, 0:1], 0.0).then_inc(s_out, 1)
            dve.memset(gu[:, 1:2], 0.0).then_inc(s_out, 1)
            dve.memset(gu[:, 2:3], 0.0).then_inc(s_out, 1)
            dve.memset(gu[:, 3:4], 0.0).then_inc(s_out, 1)
            statistics(0, 0, 0)
            high_x(0, 0, 0)
            for tap in range(TAPS):
                conv_tap(0, 0, 0, tap)
            rounds(dve, batch)


_INS = ["L0_attn_x", "L0_attn_wqkv", "L0_attn_wo", "L0_ffn_Wr", "L0_ffn_router_bias", "L0_ffn_Wg", "L0_ffn_Wu",
        "L0_ffn_Wd", "L0_ffn_conv_w", "L0_ffn_conv_b"]


def _constants():
    import numpy as np
    f = np.float32
    p = np.arange(128)
    ident = (p[:, None] == p[None, :]).astype(f)
    causal = (p[:, None] <= p[None, :]).astype(f)
    same_head = (p[:, None] // 16 == p[None, :] // 16).astype(f)
    parity = np.stack([(p // 16) % 2 == 0, (p // 16) % 2 == 1], 1).astype(f)
    rows = np.zeros((8, 4, 128), f)
    for e in range(4):
        rows[e, e] = rows[4 + e, e] = 1.0
    iota = np.broadcast_to(np.arange(8, dtype=f), (128, 4, 8)).copy()
    return {"ident": ident, "causal": causal, "same_head": same_head, "parity": parity, "expert_rows": rows,
            "iota": iota}


def kernel(**inputs):
    import numpy as _np
    import concourse.bacc as _bacc
    from concourse import mybir as _mybir
    from concourse.bass_utils import run_bass_kernel_spmd as _run

    nc = _bacc.Bacc("TRN2", target_bir_lowering=False, num_devices=1)
    arrays, args = {}, []
    given = {name: inputs[name] for name in _INS}
    given["L0_ffn_conv_w"] = _np.asarray(given["L0_ffn_conv_w"])[:, 0, :].T.reshape(2, 128, 4).transpose(1, 0, 2)
    given["L0_ffn_conv_b"] = _np.asarray(given["L0_ffn_conv_b"]).reshape(2, 128).T
    given["L0_ffn_router_bias"] = _np.broadcast_to(_np.asarray(given["L0_ffn_router_bias"]), (128, 8))
    given.update(_constants())
    for name, a in given.items():
        a = _np.ascontiguousarray(a)
        arrays[f"in_{name}_dram"] = a
        args.append(nc.dram_tensor(f"in_{name}_dram", a.shape, _mybir.dt.from_np(a.dtype), kind="ExternalInput").ap())
    shape = tuple(inputs["L0_attn_x"].shape)
    args.append(nc.dram_tensor("out_0_dram", shape, _mybir.dt.float32, kind="ExternalOutput").ap())
    layer_kernel(nc, *args)
    r = _run(nc, [arrays], core_ids=[0])
    return r.results[0]["out_0_dram"]
```

```python
from contextlib import ExitStack

import concourse.bass as bass
from concourse import mybir

F32 = mybir.dt.float32
F32R = mybir.dt.float32r
U32 = mybir.dt.uint32
ALU = mybir.AluOpType
ACT = mybir.ActivationFunctionType
AX = mybir.AxisListType

P = 128


def layer_kernel(nc, x, wqkv, wo, w_router, router_bias, w_gate, w_up, w_down, conv_w, conv_b,
                 ident, causal, same_head, parity, expert_rows, iota, out):
    n_seq, seq_len, D = x.shape
    E, _, I = w_gate.shape
    NR = w_router.shape[1]
    HD = 16
    C = D // P
    T = 4
    BT = T * P
    BPS = seq_len // BT
    TAPS = conv_w.shape[2]
    HALO = TAPS - 1
    EPS_LN, EPS_DEN, EPS_W = 1e-5, 1e-5, 1e-9
    VW = D + NR
    PAIRS = D // (2 * HD)
    PPG = PAIRS // C
    assert I == P and E == T and D == C * P and PPG == 4 and BPS == 4

    x_v = x.rearrange("s (b t p) c -> (s b) p t c", p=P, t=T)
    out_v = out.rearrange("s (b t p) c -> (s b) p t c", p=P, t=T)

    with ExitStack() as ctx:
        def sb(name, shape, dt=F32):
            return ctx.enter_context(nc.sbuf_tensor(name, shape, dt))

        def bank(name):
            return ctx.enter_context(nc.psum_tensor(name, [P, BT], F32))

        def sem(name):
            return ctx.enter_context(nc.semaphore(name))

        wqk_h, wqk_l = sb("wqk_h", [P, C, 2 * D], F32R), sb("wqk_l", [P, C, 2 * D], F32R)
        wvr_h, wvr_l = sb("wvr_h", [P, C, VW], F32R), sb("wvr_l", [P, C, VW], F32R)
        wgu_h, wgu_l = sb("wgu_h", [P, 2, E, C, I], F32R), sb("wgu_l", [P, 2, E, C, I], F32R)
        wd_h, wd_l = sb("wd_h", [P, E, D], F32R), sb("wd_l", [P, E, D], F32R)
        wo_h, wo_l = sb("wo_h", [P, C, D], F32R), sb("wo_l", [P, C, D], F32R)
        conv_ws = sb("conv_ws", [P, C, TAPS])
        conv_bs = sb("conv_bs", [P, C])
        bias_s = sb("bias_s", [P, NR])
        ident_s = sb("ident_s", [P, P])
        causal_s = sb("causal_s", [P, P])
        same_head_s = sb("same_head_s", [P, P])
        parity_s = sb("parity_s", [P, 2])
        sel = sb("sel", [2 * E, E, P], F32R)
        iota_s = sb("iota_s", [P, T, NR])
        zeros = sb("zeros", [P, BT])
        half = sb("half", [P, T])
        spare = sb("spare", [P, 1])
        x_t = sb("x_t", [P, 2, T, D])
        xn = sb("xn", [P, T, D])
        stats = sb("stats", [P, T, 6])
        mv = sb("mv", [P, T, 2])
        negm = sb("negm", [P, T])
        vare = sb("vare", [P, T])
        rstd = sb("rstd", [P, T])
        xT = sb("xT", [P, C, HALO + BT])
        xh, xl = sb("xh", [P, C, BT], F32R), sb("xl", [P, C, BT], F32R)
        kT = sb("kT", [P, C, BT])
        kh, kl = sb("kh", [P, C, BT], F32R), sb("kl", [P, C, BT], F32R)
        qT = sb("qT", [P, C, BT])
        qh, ql = sb("qh", [P, C, 2, BT], F32R), sb("ql", [P, C, 2, BT], F32R)
        ksum = sb("ksum", [P, 2, C, BT])
        qks = sb("qks", [P, C, BT])
        den = sb("den", [P, C, BT])
        rden = sb("rden", [P, 2, C, P])
        vp = sb("vp", [P, T, PAIRS, 3, HD])
        score = sb("score", [P, T, NR])
        scoreb = sb("scoreb", [P, T, NR])
        top = sb("top", [P, T, 8])
        topi = sb("topi", [P, T, 8], U32)
        hot = sb("hot", [P, 2, T, NR])
        picked = sb("picked", [P, T, NR])
        wsum = sb("wsum", [P, 3, T])
        cw = sb("cw", [P, T, NR])
        c46 = sb("c46", [P, T, 1])
        cws = sb("cws", [P, T, 2 * E], F32R)
        cwT = sb("cwT", [2 * E, BT], F32R)
        sm = sb("sm", [P, 2, 2 * PAIRS, P])
        ktok = sb("ktok", [P, D])
        state = sb("state", [P, D])
        state_bd = sb("state_bd", [P, D])
        yT = sb("yT", [P, C, BT])
        yh, yl = sb("yh", [P, C, BT], F32R), sb("yl", [P, C, BT], F32R)
        sg = sb("sg", [P, 2, BT])
        gu = sb("gu", [P, BT])
        hid = sb("hid", [P, E, BT])
        hh, hl = sb("hh", [P, E, BT], F32R), sb("hl", [P, E, BT], F32R)
        cT = sb("cT", [P, 2, C, BT])

        same = qks[:, :, :].rearrange("p c n -> p (c n)").rearrange("p (t d) -> p t d", t=T)

        st_qkv = hid[:, :, :].rearrange("p e n -> p (e n)")[:, 0:C * 3 * D].rearrange("p (c n) -> p c n", c=C)
        st_g = sm[:, 0, 0:8, :].rearrange("p h n -> p (h n)").rearrange("p (e c i) -> p e c i", e=E, c=C)
        st_u = sm[:, 0, 8:16, :].rearrange("p h n -> p (h n)").rearrange("p (e c i) -> p e c i", e=E, c=C)
        st_d = qT[:, :, :].rearrange("p c n -> p (c n)").rearrange("p (e n) -> p e n", e=E)
        st_o = ksum[:, 0, 0, :].rearrange("p (c n) -> p c n", c=C)
        st_r = ksum[:, 0, 1, 0:C * NR].rearrange("p (c n) -> p c n", c=C)
        st_sel = ksum[0:2 * E, 1, 0, 0:E * P].rearrange("p (e n) -> p e n", e=E)

        R = [bank(f"ring{k}") for k in range(3)]
        SB = [bank(f"scores{k}") for k in range(2)]
        NUM, TR, ST = bank("num"), bank("turned"), bank("state_add")
        VB = R + [TR]
        KB, QB = [NUM, ST], SB
        XB = [R[0], R[1]]

        w_in = sem("w_in")
        w_split = sem("w_split")
        w_hi = sem("w_hi")
        set_up = sem("set_up")
        x_in = [sem("x_in0"), sem("x_in1")]
        stored = [sem("stored0"), sem("stored1")]
        s_stats = sem("s_stats")
        s_rstd = sem("s_rstd")
        s_xn = sem("s_xn")
        s_xtr = sem("s_xtr")
        s_xT = sem("s_xT")
        s_halo = sem("s_halo")
        s_xh = sem("s_xh")
        s_xl = sem("s_xl")
        s_kp = sem("s_kp")
        s_kT = sem("s_kT")
        s_kh = sem("s_kh")
        s_kl = sem("s_kl")
        s_qp = sem("s_qp")
        s_qT = sem("s_qT")
        s_qh = sem("s_qh")
        s_ql = sem("s_ql")
        s_vp = sem("s_vp")
        s_v = sem("s_v")
        s_sig = sem("s_sig")
        s_cw = sem("s_cw")
        s_cws = sem("s_cws")
        s_cwtr = sem("s_cwtr")
        s_cwT = sem("s_cwT")
        s_qks = sem("s_qks")
        s_denp = sem("s_denp")
        s_den = sem("s_den")
        s_gp = sem("s_gp")
        s_sg = sem("s_sg")
        s_up = sem("s_up")
        s_gu = sem("s_gu")
        s_cwp = sem("s_cwp")
        s_hid = sem("s_hid")
        s_hh = sem("s_hh")
        s_hl = sem("s_hl")
        s_s = sem("s_s")
        s_sm = sem("s_sm")
        s_ktr = sem("s_ktr")
        s_ktok = sem("s_ktok")
        s_num = sem("s_num")
        s_y = sem("s_y")
        s_yh = sem("s_yh")
        s_yl = sem("s_yl")
        s_st = sem("s_st")
        s_state = sem("s_state")
        s_bd = sem("s_bd")
        s_conv = sem("s_conv")
        s_base1 = sem("s_base1")
        s_same = sem("s_same")
        s_relu7 = sem("s_relu7")
        s_base2 = sem("s_base2")
        s_op = sem("s_op")
        s_out = sem("s_out")
        s_own = sem("s_own")

        N_BATCH = n_seq * BPS
        LOADS = [0]

        def rounds(engine, body):
            with engine.Fori(0, n_seq - 1) as s:
                for j in range(BPS):
                    body(s, j, BPS)
            for j in range(BPS):
                body(n_seq - 1, j, BPS - 1 - j)

        def at(s, j, per, k):
            return s * (BPS * per) + (j * per + k)

        SPLITS = [("qk", wqk_h[:, c, :], wqk_l[:, c, :], st_qkv[:, c, 0:2 * D]) for c in range(C)]
        SPLITS += [("v", wvr_h[:, c, 0:D], wvr_l[:, c, 0:D], st_qkv[:, c, 2 * D:3 * D]) for c in range(C)]
        SPLITS += [("router", wvr_h[:, :, D:VW], wvr_l[:, :, D:VW], st_r)]
        SPLITS += [("gate", wgu_h[:, 0], wgu_l[:, 0], st_g), ("up", wgu_h[:, 1], wgu_l[:, 1], st_u)]
        SPLITS += [("down", wd_h[:, :, :], wd_l[:, :, :], st_d), ("out", wo_h[:, :, :], wo_l[:, :, :], st_o)]
        N_SPLITS = len(SPLITS)
        OWN_SETUP = 2 + (TAPS - 1)
        OWN_BATCH = 1 + 11 + T + 2 + (TAPS - 1)

        def settled(engine):
            engine.wait_ge(set_up, 4)

        block = ctx.enter_context(nc.Block())

        @block.sync
        def _(sp):
            def load(dst, src):
                sp.dma_start(dst, src).then_inc(w_in, 16)
                LOADS[0] += 1
            sp.dma_start(x_t[:, 0], x_v[0]).then_inc(x_in[0], 16)
            for c in range(C):
                load(st_qkv[:, c, :], wqkv[c * P:(c + 1) * P, :])
                load(st_o[:, c, :], wo[c * P:(c + 1) * P, :])
                load(st_r[:, c, :], w_router[c * P:(c + 1) * P, :])
            load(conv_ws[:, :, :], conv_w)
            load(conv_bs[:, :], conv_b)
            for src, dst in ((w_gate, st_g), (w_up, st_u)):
                for c in range(C):
                    load(dst[:, :, c, :], src[:, c * P:(c + 1) * P, :].rearrange("e p i -> p e i"))
            load(st_d, w_down.rearrange("e p n -> p e n"))
            load(bias_s[:, :], router_bias)
            load(ident_s[:, :], ident)
            load(causal_s[:, :], causal)
            load(same_head_s[:, :], same_head)
            load(parity_s[:, :], parity)
            load(st_sel, expert_rows)
            load(iota_s[:, :, :], iota)
            sp.dma_start(x_t[:, 1], x_v[1]).then_inc(x_in[1], 16)

            def batch(s, j, left):
                b = s * BPS + j
                sp.wait_ge(s_out, at(s, j, T, 2 * T))
                sp.dma_start(out_v[b], x_t[:, j % 2]).then_inc(stored[j % 2], 16)
                if left < 2:
                    return
                sp.wait_ge(stored[j % 2], s * (BPS // 2 * 16) + (j // 2 + 1) * 16)
                sp.dma_start(x_t[:, j % 2], x_v[b + 2]).then_inc(x_in[j % 2], 16)

            rounds(sp, batch)
            for p in range(2):
                sp.wait_ge(stored[p], N_BATCH // 2 * 16)

        N_LOADS = LOADS[0]

        @block.tensor
        def _(pe):
            mm = nc.tensor.matmul

            def turn_xn(s, j, k):
                pe.wait_ge(s_xn, at(s, j, 1, k + 1))
                for c in range(C):
                    if k and c == 0:
                        pe.wait_ge(s_sg, at(s, j, T, T))
                    elif k:
                        pe.wait_ge(s_gu, at(s, j, T, T))
                    for t in range(T):
                        ins = nc.tensor.transpose(XB[c][:, t * P:(t + 1) * P], xn[:, t, c * P:(c + 1) * P],
                                                  ident_s[:, :])
                    ins.then_inc(s_xtr, 1)

            def product(dst, pairs, first=True, final=True):
                passes = [q for lh, ll, rh, rl in pairs for q in ((lh, rl), (lh, rh), (ll, rh))]
                for n, (lhs, rhs) in enumerate(passes):
                    ins = mm(dst, lhs, rhs, start=first and n == 0, stop=final and n == len(passes) - 1,
                             skip_group_check=not first)
                return ins

            def batch(s, j, left):
                last = left == 0
                pe.wait_ge(s_xh, at(s, j, C, C))
                pe.wait_ge(s_xl, at(s, j, C, C))

                def project(dst, h, l, col):
                    return product(dst, [(h[:, c, col:col + P], l[:, c, col:col + P], xh[:, c, :], xl[:, c, :])
                                         for c in range(C)])

                for t in range(T):
                    if t < 3:
                        pe.wait_ge(s_out, at(s, j, T, 2 + t))
                    ts = slice(t * P, (t + 1) * P)
                    product(VB[t][:, 0:VW], [(xh[:, c, ts], xl[:, c, ts], wvr_h[:, c, :], wvr_l[:, c, :])
                                                for c in range(C)]).then_inc(s_vp, 1)
                for g in range(C):
                    project(KB[g][:, :], wqk_h, wqk_l, D + g * P).then_inc(s_kp, 1)
                for g in range(C):
                    project(QB[g][:, :], wqk_h, wqk_l, g * P).then_inc(s_qp, 1)

                def scores(t, fs):
                    if t or fs[0]:
                        pe.wait_ge(s_sm, at(s, j, 16, 4 * t + fs[0]))
                    ts = slice(t * P, (t + 1) * P)
                    for g in range(C):
                        for n, (k, q) in enumerate(((kh, ql), (kh, qh), (kl, qh))):
                            for f in fs:
                                rows = slice(32 * f, 32 * f + 32)
                                ins = mm(SB[f % 2][:, g * 2 * P:(g + 1) * 2 * P], k[rows, g, ts], q[rows, g, :, ts],
                                         start=n == 0, stop=n == 2)
                    ins.then_inc(s_s, 1)

                def gate(t, u):
                    product(R[u][:, :], [((wgu_h[:, u, t, c, :]), wgu_l[:, u, t, c, :], xh[:, c, :], xl[:, c, :])
                                         for c in range(C)]).then_inc(s_up if u else s_gp, 1)

                def denominator(g):
                    pe.wait_ge(s_qks, at(s, j, C, g + 1))
                    if g == 1:
                        pe.wait_ge(s_sg, at(s, j, T, 1))
                    mm(R[2 - 2 * g][:, :], same_head_s[:, :], qks[:, g, :], start=True, stop=True).then_inc(s_denp, 1)

                def numerators(t):
                    ts = slice(t * P, (t + 1) * P)
                    if t:
                        pe.wait_ge(s_y, at(s, j, T, t))
                    first_tile = j == 0 and t == 0
                    if not first_tile:
                        pe.wait_ge(s_bd, at(s, j, T, t))
                    for g in range(C):
                        gs = slice(g * P, (g + 1) * P)
                        if not first_tile:
                            mm(NUM[:, gs], state_bd[:, gs], qT[:, g, ts], start=True, stop=False)
                        pe.wait_ge(s_sm, at(s, j, 16, 4 * t + 4))
                        for par in range(2):
                            for m in range(PPG):
                                pair = g * PPG + m
                                window = vp[:, t, pair, par:par + 2, :].rearrange("p a d -> p (a d)")
                                ins = mm(NUM[32 * m:32 * m + 32, gs], window, sm[:, t % 2, 2 * pair + par, :],
                                         start=first_tile and par == 0, stop=par == 1)
                    ins.then_inc(s_num, 1)
                    pe.wait_ge(s_ktok, at(s, j, T, t + 1))
                    if t:
                        pe.wait_ge(s_state, at(s, j, T, t))
                    for g in range(C):
                        gs = slice(g * P, (g + 1) * P)
                        ins = mm(ST[:, gs], ktok[:, gs], vp[:, t, g * PPG:(g + 1) * PPG, 0:3:2, :],
                                 start=True, stop=True)
                    ins.then_inc(s_st, 1)

                def small(t):
                    if t == 0:
                        pe.wait_ge(s_cwT, at(s, j, 1, 1))
                    else:
                        pe.wait_ge(s_ktok, at(s, j, T, t))
                    ts = slice(t * P, (t + 1) * P)
                    for g in range(C):
                        ins = nc.tensor.transpose(TR[:, g * P:(g + 1) * P], kT[:, g, ts], ident_s[:, :])
                    ins.then_inc(s_ktr, 1)
                    if t == 0:
                        pe.wait_ge(s_den, at(s, j, C, 1))
                    else:
                        pe.wait_ge(s_hid, at(s, j, T, t))
                    mm(R[2][:, :], sel[:, t, :], cwT[:, :], start=True, stop=True).then_inc(s_cwp, 1)

                pe.wait_ge(w_split, N_SPLITS)
                pe.wait_ge(s_sig, at(s, j, T, 1))
                gate(0, 0)
                pe.wait_ge(s_sig, at(s, j, T, 2))
                gate(0, 1)
                pe.wait_ge(s_cws, at(s, j, 1, 1))
                for t in range(T):
                    ins = nc.tensor.transpose(TR[0:2 * E, t * P:(t + 1) * P], cws[:, t, :].bitcast(F32), ident_s[:, :])
                ins.then_inc(s_cwtr, 1)
                denominator(0)
                pe.wait_ge(s_kl, at(s, j, C, C))
                pe.wait_ge(s_ql, at(s, j, C, C))
                for t in range(T):
                    scores(t, (0, 1))
                    if t == 0:
                        denominator(1)
                        small(t)
                    else:
                        numerators(t - 1)
                        pe.wait_ge(s_gu, at(s, j, T, t))
                        gate(t, 1)
                    scores(t, (2, 3))
                    if t > 0:
                        small(t)
                    if t < T - 1:
                        if t == 0:
                            pe.wait_ge(s_den, at(s, j, C, 2))
                        else:
                            pe.wait_ge(s_sg, at(s, j, T, t + 1))
                        gate(t + 1, 0)
                    elif not last:
                        turn_xn(s, j, 1)
                numerators(T - 1)

                for t in range(T):
                    ts = slice(t * P, (t + 1) * P)
                    bank_o = R[(t + 2) % 3]
                    if t == 0:
                        pe.wait_ge(s_hid, at(s, j, T, T))
                        pe.wait_ge(s_conv, at(s, j, 1, 1))
                    elif t == 1:
                        if last:
                            pe.wait_ge(s_sg, at(s, j, T, T))
                        else:
                            pe.wait_ge(s_xT, at(s, j, C, C + 1))
                    elif t == 2:
                        if last:
                            pe.wait_ge(s_gu, at(s, j, T, T))
                        else:
                            pe.wait_ge(s_xT, at(s, j, C, 2 * C))
                    else:
                        pe.wait_ge(s_out, at(s, j, T, T + 1))
                    for c in range(C):
                        mm(bank_o[:, c * P:(c + 1) * P], cT[:, j % 2, c, ts], ident_s[:, :], is_transpose=True,
                           start=c == 0, stop=False, skip_group_check=True)
                    pe.wait_ge(s_yh, at(s, j, T, t + 1))
                    pe.wait_ge(s_yl, at(s, j, T, t + 1))
                    product(bank_o[:, 0:D], [(yh[:, c, ts], yl[:, c, ts], wo_h[:, c, :], wo_l[:, c, :])
                                             for c in range(C)], first=False, final=False)
                    for e in range(E):
                        if t == 0:
                            pe.wait_ge(s_hh, at(s, j, T, e + 1))
                            pe.wait_ge(s_hl, at(s, j, T, e + 1))
                        ins = product(bank_o[:, 0:D], [(hh[:, e, ts], hl[:, e, ts], wd_h[:, e, :], wd_l[:, e, :])],
                                      first=False, final=e == E - 1)
                    ins.then_inc(s_op, 1)

            pe.wait_ge(w_in, 16 * N_LOADS)
            turn_xn(0, 0, 0)
            pe.wait_ge(w_split, N_SPLITS)
            pe.wait_ge(set_up, 4)
            rounds(pe, batch)

        @block.scalar
        def _(act):
            copy = lambda o, i: nc.scalar.activation(o, i, ACT.Copy)
            act.wait_ge(w_in, 16 * N_LOADS)
            for _, hi, _, src in SPLITS:
                copy(hi, src).then_inc(w_hi, 1)
            copy(sel[:, :, :], st_sel).then_inc(set_up, 1)

            def fill_xT(s, j, k):
                if k:
                    act.wait_ge(s_conv, at(s, j, 1, 1))
                if k and j < BPS - 1:
                    act.activation(xT[:, :, 0:HALO], xT[:, :, BT:BT + HALO], ACT.Copy).then_inc(s_halo, 1)
                else:
                    act.activation(xT[:, :, 0:HALO], zeros[:, 0:C * HALO].rearrange("p (c h) -> p c h", c=C),
                                   ACT.Copy).then_inc(s_halo, 1)
                act.wait_ge(s_halo, at(s, j, 1, k + 1))
                for c in range(C):
                    act.wait_ge(s_xtr, at(s, j, C, k * C + c + 1))
                    copy(xT[:, c, HALO:HALO + BT], XB[c][:, :]).then_inc(s_xT, 1)

            def batch(s, j, left):
                last = left == 0
                def high_y(t):
                    act.wait_ge(s_y, at(s, j, T, t + 1))
                    ts = slice(t * P, (t + 1) * P)
                    copy(yh[:, :, ts], yT[:, :, ts]).then_inc(s_yh, 1)

                for t in range(T):
                    act.wait_ge(s_vp, at(s, j, T, t + 1))
                    copy(vp[:, t, :, 0:3:2, :],
                         VB[t][:, 0:D].rearrange("p (a b d) -> p a b d", a=PAIRS, b=2)).then_inc(s_v, 1)
                    act.activation(score[:, t, :], VB[t][:, D:VW], ACT.Sigmoid).then_inc(s_sig, 1)
                for g in range(C):
                    act.wait_ge(s_kp, at(s, j, C, g + 1))
                    act.activation(kT[:, g, :], KB[g][:, :], ACT.Relu).then_inc(s_kT, 1)
                    act.wait_ge(s_kT, at(s, j, C, g + 1))
                    copy(kh[:, g, :], kT[:, g, :]).then_inc(s_kh, 1)
                for g in range(C):
                    act.wait_ge(s_qp, at(s, j, C, g + 1))
                    act.activation(qT[:, g, :], QB[g][:, :], ACT.Relu).then_inc(s_qT, 1)
                    act.wait_ge(s_qT, at(s, j, C, g + 1))
                    for par in range(2):
                        ins = act.activation(qh[:, g, par, :], qT[:, g, :], ACT.Copy, scale=parity_s[:, par:par + 1])
                    ins.then_inc(s_qh, 1)
                for t in range(T):
                    act.wait_ge(s_gp, at(s, j, T, t + 1))
                    act.activation(sg[:, t % 2, :], R[0][:, :], ACT.Silu).then_inc(s_sg, 1)
                    if t == 0:
                        act.wait_ge(s_cwtr, at(s, j, 1, 1))
                        copy(cwT[:, :], TR[0:2 * E, :]).then_inc(s_cwT, 1)
                        for g in range(C):
                            act.wait_ge(s_denp, at(s, j, C, g + 1))
                            act.activation(den[:, g, :], R[2 - 2 * g][:, :], ACT.Copy, bias=EPS_DEN).then_inc(s_den, 1)
                    act.wait_ge(s_ktr, at(s, j, T, t + 1))
                    copy(ktok[:, :], TR[:, 0:D]).then_inc(s_ktok, 1)
                    if t:
                        high_y(t - 1)
                    act.wait_ge(s_hid, at(s, j, T, t + 1))
                    copy(hh[:, t, :], hid[:, t, :]).then_inc(s_hh, 1)
                    if t == 0:
                        act.wait_ge(s_cw, at(s, j, 1, 1))
                        for tt in range(T):
                            ins = act.activation(same[:, tt, :], xn[:, tt, :], ACT.Copy, scale=c46[:, tt, :])
                        ins.then_inc(s_same, 1)
                    if t == 1:
                        act.wait_ge(s_same, at(s, j, 1, 1))
                        for tt in range(T):
                            ins = act.activation(xn[:, tt, :], xn[:, tt, :], ACT.Relu, scale=cw[:, tt, NR - 1:NR])
                        ins.then_inc(s_relu7, 1)
                if not last:
                    fill_xT(s, j, 1)
                high_y(T - 1)

            act.wait_ge(set_up, 4)
            fill_xT(0, 0, 0)
            rounds(act, batch)

        @block.gpsimd
        def _(pool):
            pool.memset(zeros[:, :], 0.0).then_inc(set_up, 1)
            pool.memset(half[:, :], -0.5).then_inc(set_up, 1)
            pool.memset(vp[:, :, :, :, :], 0.0).then_inc(set_up, 1)

            def normalise(s, j, k):
                pool.wait_ge(s_stats, at(s, j, 1, k + 1))
                pool.tensor_tensor(rstd[:, :], vare[:, :], half[:, :], ALU.pow).then_inc(s_rstd, 1)
                settled(pool)
                pool.wait_ge(s_rstd, at(s, j, 1, k + 1))
                for t in range(T):
                    ins = pool.tensor_scalar(xn[:, t, :], x_t[:, (j + k) % 2, t, :], negm[:, t:t + 1],
                                             rstd[:, t:t + 1], ALU.add, ALU.mult)
                ins.then_inc(s_xn, 1)

            def low_x(s, j, k):
                for c in range(C):
                    pool.wait_ge(s_xh, at(s, j, C, k * C + c + 1))
                    pool.tensor_tensor(xl[:, c, :], xT[:, c, HALO:HALO + BT], xh[:, c, :].bitcast(F32),
                                       ALU.subtract).then_inc(s_xl, 1)

            def batch(s, j, left):
                last = left == 0
                xb = x_t[:, j % 2, :, :]
                for g in range(C):
                    pool.wait_ge(s_kh, at(s, j, C, g + 1))
                    pool.tensor_tensor(kl[:, g, :], kT[:, g, :], kh[:, g, :].bitcast(F32),
                                       ALU.subtract).then_inc(s_kl, 1)
                def keep_blocks(t):
                    pool.wait_ge(s_state, at(s, j, T, t + 1))
                    for g in range(C):
                        gs = slice(g * P, (g + 1) * P)
                        ins = pool.tensor_tensor(state_bd[:, gs], state[:, gs], same_head_s[:, :], ALU.mult)
                    ins.then_inc(s_bd, 1)

                def low_y(t):
                    ts = slice(t * P, (t + 1) * P)
                    pool.wait_ge(s_yh, at(s, j, T, t + 1))
                    pool.tensor_tensor(yl[:, :, ts], yT[:, :, ts], yh[:, :, ts].bitcast(F32),
                                       ALU.subtract).then_inc(s_yl, 1)

                for t in range(T):
                    if t:
                        keep_blocks(t - 1)
                        low_y(t - 1)
                    pool.wait_ge(s_hh, at(s, j, T, t + 1))
                    pool.tensor_tensor(hl[:, t, :], hid[:, t, :], hh[:, t, :].bitcast(F32),
                                       ALU.subtract).then_inc(s_hl, 1)
                    if t == 0:
                        pool.wait_ge(s_same, at(s, j, 1, 1))
                        pool.tensor_tensor(xb, xb, same[:, :, :], ALU.add).then_inc(s_base1, 1)
                    if t == 1:
                        pool.wait_ge(s_base1, at(s, j, 1, 1))
                        pool.wait_ge(s_relu7, at(s, j, 1, 1))
                        pool.tensor_tensor(xb, xb, xn[:, :, :], ALU.add).then_inc(s_base2, 1)
                    if t == 1 and not last:
                        pool.wait_ge(s_base2, at(s, j, 1, 1))
                        normalise(s, j, 1)
                low_y(T - 1)
                if not last:
                    low_x(s, j, 1)
                    keep_blocks(T - 1)

            pool.wait_ge(set_up, 4)
            normalise(0, 0, 0)
            low_x(0, 0, 0)
            rounds(pool, batch)

        @block.vector
        def _(dve):
            def statistics(s, j, k):
                p = (j + k) % 2
                dve.wait_ge(x_in[p], s * (BPS // 2 * 16) + ((j + k) // 2 + 1) * 16)
                for t in range(T):
                    ins = dve.bn_stats(stats[:, t, :], x_t[:, p, t, :])
                own(ins, s, j, apart=True)
                for t in range(T):
                    ins = dve.bn_aggr(mv[:, t, :], stats[:, t, :])
                own(ins, s, j)
                dve.tensor_scalar(negm[:, :], mv[:, :, 0], -1.0, None, ALU.mult)
                dve.tensor_scalar(vare[:, :], mv[:, :, 1], EPS_LN, None, ALU.add).then_inc(s_stats, 1)

            count = {"setup": 0, "batch": 0, "in_batch": False}

            def own(ins, s, j, apart=False):
                ins.then_inc(s_own, 1)
                if not count["in_batch"]:
                    count["setup"] += 1
                    dve.wait_ge(s_own, count["setup"])
                    return
                count["batch"] += 1
                dve.wait_ge(s_own, s * (BPS * OWN_BATCH) + (j * OWN_BATCH + count["batch"] + OWN_SETUP))
                if apart:
                    dve.memset(spare[:, :], 0.0)

            def high_x(s, j, k):
                for c in range(C):
                    dve.wait_ge(s_xT, at(s, j, C, k * C + c + 1))
                    dve.tensor_copy(xh[:, c, :], xT[:, c, HALO:HALO + BT]).then_inc(s_xh, 1)

            def router(s, j):
                dve.wait_ge(s_sig, at(s, j, T, T))
                bias_b = bias_s[:, :].unsqueeze(1).to_broadcast([P, T, NR])
                own(dve.tensor_tensor(scoreb[:, :, :], score[:, :, :], bias_b, ALU.add), s, j, apart=True)
                for t in range(T):
                    ins = dve.max(top[:, t, :], scoreb[:, t, :])
                own(ins, s, j, apart=True)
                for t in range(T):
                    ins = dve.max_index(topi[:, t, :], top[:, t, :], scoreb[:, t, :])
                own(ins, s, j)
                for n in range(2):
                    ins = dve.tensor_tensor(hot[:, n, :, :], iota_s[:, :, :],
                                            topi[:, :, n:n + 1].to_broadcast([P, T, NR]), ALU.is_equal)
                own(ins, s, j)
                own(dve.tensor_tensor(hot[:, 0, :, :], hot[:, 0, :, :], hot[:, 1, :, :], ALU.add), s, j)
                own(dve.tensor_tensor(picked[:, :, :], hot[:, 0, :, :], score[:, :, :], ALU.mult), s, j)
                own(dve.tensor_reduce(wsum[:, 0, :], picked[:, :, :], AX.X, ALU.add), s, j)
                own(dve.tensor_scalar(wsum[:, 1, :], wsum[:, 0, :], EPS_W, None, ALU.add), s, j)
                own(dve.reciprocal(wsum[:, 2, :], wsum[:, 1, :]), s, j)
                own(dve.tensor_tensor(cw[:, :, :], picked[:, :, :],
                                      wsum[:, 2, :].unsqueeze(2).to_broadcast([P, T, NR]), ALU.mult), s, j)
                own(dve.tensor_copy(cws[:, :, 0:E], cw[:, :, 0:E]), s, j)
                dve.tensor_tensor(cws[:, :, E:2 * E], cw[:, :, 0:E], cws[:, :, 0:E].bitcast(F32),
                                  ALU.subtract).then_inc(s_cws, 1)
                dve.tensor_tensor(c46[:, :, :], cw[:, :, E:E + 1], cw[:, :, E + 2:E + 3], ALU.add).then_inc(s_cw, 1)

            def conv_tap(s, j, k, tap):
                for c in range(C):
                    src, dst = xT[:, c, tap:tap + BT], cT[:, (j + k) % 2, c, :]
                    if tap == 0:
                        ins = dve.tensor_scalar(dst, src, conv_ws[:, c, 0:1], conv_bs[:, c:c + 1], ALU.mult, ALU.add)
                    else:
                        ins = dve.scalar_tensor_tensor(out=dst, in0=src, scalar=conv_ws[:, c, tap:tap + 1],
                                                       in1=dst, op0=ALU.mult, op1=ALU.add)
                if tap < TAPS - 1:
                    own(ins, s, j)
                else:
                    ins.then_inc(s_conv, 1)

            def batch(s, j, left):
                last = left == 0
                count["batch"], count["in_batch"] = 0, True
                router(s, j)
                for g in range(C):
                    dve.wait_ge(s_kT, at(s, j, C, g + 1))
                    before = ksum[:, (j + 1) % 2, g, BT - 1:BT] if j else 0.0
                    ins = dve.tensor_tensor_scan(ksum[:, j % 2, g, :], kT[:, g, :], zeros[:, :], before,
                                                 ALU.add, ALU.add)
                own(ins, s, j)
                for g in range(C):
                    dve.wait_ge(s_qT, at(s, j, C, g + 1))
                    dve.tensor_tensor(qks[:, g, :], qT[:, g, :], ksum[:, j % 2, g, :], ALU.mult).then_inc(s_qks, 1)
                    dve.wait_ge(s_qh, at(s, j, C, g + 1))
                    for par in range(2):
                        ins = dve.scalar_tensor_tensor(out=ql[:, g, par, :], in0=qT[:, g, :],
                                                       scalar=parity_s[:, par:par + 1],
                                                       in1=qh[:, g, par, :].bitcast(F32),
                                                       op0=ALU.mult, op1=ALU.subtract)
                    ins.then_inc(s_ql, 1)

                def mask(t, f):
                    dve.wait_ge(s_s, at(s, j, 8, 2 * t + f // 2 + 1))
                    heads = sm[:, t % 2, :, :].rearrange("p (g m a) n -> p g m (a n)", g=C, a=2)[:, :, f, :]
                    dve.tensor_tensor(heads.rearrange("p g (a n) -> p g a n", a=2),
                                      SB[f % 2][:, :].rearrange("p (g a n) -> p g a n", g=C, a=2),
                                      causal_s[:, :].unsqueeze(1).unsqueeze(1).to_broadcast([P, C, 2, P]),
                                      ALU.mult).then_inc(s_sm, 1)

                def gate_up(t):
                    dve.wait_ge(s_sg, at(s, j, T, t + 1))
                    dve.wait_ge(s_up, at(s, j, T, t + 1))
                    dve.tensor_tensor(gu[:, :], R[1][:, :], sg[:, t % 2, :], ALU.mult).then_inc(s_gu, 1)

                def invert(t):
                    dve.wait_ge(s_den, at(s, j, C, C))
                    own(dve.reciprocal(rden[:, t % 2], den[:, :, t * P:(t + 1) * P]), s, j)

                def attend(t):
                    ts = slice(t * P, (t + 1) * P)
                    dve.wait_ge(s_num, at(s, j, T, t + 1))
                    dve.tensor_tensor(yT[:, :, ts], NUM[:, 0:D].rearrange("p (g n) -> p g n", g=C), rden[:, t % 2],
                                      ALU.mult).then_inc(s_y, 1)
                    dve.wait_ge(s_st, at(s, j, T, t + 1))
                    if j == 0 and t == 0:
                        dve.tensor_copy(state[:, :], ST[:, 0:D]).then_inc(s_state, 1)
                    else:
                        dve.tensor_tensor(state[:, :], ST[:, 0:D], state[:, :], ALU.add).then_inc(s_state, 1)

                for t in range(T):
                    if t == 0:
                        gate_up(t)
                    mask(t, 0)
                    mask(t, 1)
                    if t > 0:
                        attend(t - 1)
                        invert(t)
                        gate_up(t)
                    mask(t, 2)
                    mask(t, 3)
                    dve.wait_ge(s_gu, at(s, j, T, t + 1))
                    dve.wait_ge(s_cwp, at(s, j, T, t + 1))
                    dve.tensor_tensor(hid[:, t, :], R[2][:, :], gu[:, :], ALU.mult).then_inc(s_hid, 1)
                    if t == 0:
                        invert(t)
                    if t == 1 and not last:
                        statistics(s, j, 1)
                attend(T - 1)
                if not last:
                    high_x(s, j, 1)
                dve.wait_ge(s_base2, at(s, j, 1, 1))
                for t in range(T):
                    dve.wait_ge(s_op, at(s, j, T, t + 1))
                    xb = x_t[:, j % 2, t, :]
                    dve.tensor_tensor(xb, R[(t + 2) % 3][:, 0:D], xb, ALU.add).then_inc(s_out, 1)
                    if not last:
                        conv_tap(s, j, 1, t)
                if not last:
                    assert count["batch"] == OWN_BATCH, count

            dve.wait_ge(w_in, 16 * N_LOADS)
            for n, (_, hi, lo, src) in enumerate(SPLITS):
                dve.wait_ge(w_hi, n + 1)
                dve.tensor_tensor(lo, src, hi.bitcast(F32), ALU.subtract).then_inc(w_split, 1)
            dve.memset(gu[:, 0:1], 0.0).then_inc(s_out, 1)
            dve.memset(gu[:, 1:2], 0.0).then_inc(s_out, 1)
            dve.memset(gu[:, 2:3], 0.0).then_inc(s_out, 1)
            dve.memset(gu[:, 3:4], 0.0).then_inc(s_out, 1)
            statistics(0, 0, 0)
            high_x(0, 0, 0)
            for tap in range(TAPS):
                conv_tap(0, 0, 0, tap)
            rounds(dve, batch)


_INS = ["L0_attn_x", "L0_attn_wqkv", "L0_attn_wo", "L0_ffn_Wr", "L0_ffn_router_bias", "L0_ffn_Wg", "L0_ffn_Wu",
        "L0_ffn_Wd", "L0_ffn_conv_w", "L0_ffn_conv_b"]


def _constants():
    import numpy as np
    f = np.float32
    p = np.arange(128)
    ident = (p[:, None] == p[None, :]).astype(f)
    causal = (p[:, None] <= p[None, :]).astype(f)
    same_head = (p[:, None] // 16 == p[None, :] // 16).astype(f)
    parity = np.stack([(p // 16) % 2 == 0, (p // 16) % 2 == 1], 1).astype(f)
    rows = np.zeros((8, 4, 128), f)
    for e in range(4):
        rows[e, e] = rows[4 + e, e] = 1.0
    iota = np.broadcast_to(np.arange(8, dtype=f), (128, 4, 8)).copy()
    return {"ident": ident, "causal": causal, "same_head": same_head, "parity": parity, "expert_rows": rows,
            "iota": iota}


def kernel(**inputs):
    import numpy as _np
    import concourse.bacc as _bacc
    from concourse import mybir as _mybir
    from concourse.bass_utils import run_bass_kernel_spmd as _run

    nc = _bacc.Bacc("TRN2", target_bir_lowering=False, num_devices=1)
    arrays, args = {}, []
    given = {name: inputs[name] for name in _INS}
    given["L0_ffn_conv_w"] = _np.asarray(given["L0_ffn_conv_w"])[:, 0, :].T.reshape(2, 128, 4).transpose(1, 0, 2)
    given["L0_ffn_conv_b"] = _np.asarray(given["L0_ffn_conv_b"]).reshape(2, 128).T
    given["L0_ffn_router_bias"] = _np.broadcast_to(_np.asarray(given["L0_ffn_router_bias"]), (128, 8))
    given.update(_constants())
    for name, a in given.items():
        a = _np.ascontiguousarray(a)
        arrays[f"in_{name}_dram"] = a
        args.append(nc.dram_tensor(f"in_{name}_dram", a.shape, _mybir.dt.from_np(a.dtype), kind="ExternalInput").ap())
    shape = tuple(inputs["L0_attn_x"].shape)
    args.append(nc.dram_tensor("out_0_dram", shape, _mybir.dt.float32, kind="ExternalOutput").ap())
    layer_kernel(nc, *args)
    r = _run(nc, [arrays], core_ids=[0])
    return r.results[0]["out_0_dram"]
```

```python
from contextlib import ExitStack

import concourse.bass as bass
from concourse import mybir

F32 = mybir.dt.float32
F32R = mybir.dt.float32r
U32 = mybir.dt.uint32
ALU = mybir.AluOpType
ACT = mybir.ActivationFunctionType
AX = mybir.AxisListType

P = 128


def layer_kernel(nc, x, wqkv, wo, w_router, router_bias, w_gate, w_up, w_down, conv_w, conv_b,
                 tables, expert_rows, out):
    n_seq, seq_len, D = x.shape
    E, _, I = w_gate.shape
    NR = w_router.shape[1]
    HD = 16
    C = D // P
    T = 4
    BT = T * P
    BPS = seq_len // BT
    TAPS = conv_w.shape[2]
    HALO = TAPS - 1
    EPS_LN, EPS_DEN, EPS_W = 1e-5, 1e-5, 1e-9
    VW = D + NR
    PAIRS = D // (2 * HD)
    PPG = PAIRS // C
    assert I == P and E == T and D == C * P and PPG == 4 and BPS == 4

    x_v = x.rearrange("s (b t p) c -> (s b) p t c", p=P, t=T)
    out_v = out.rearrange("s (b t p) c -> (s b) p t c", p=P, t=T)

    with ExitStack() as ctx:
        def sb(name, shape, dt=F32):
            return ctx.enter_context(nc.sbuf_tensor(name, shape, dt))

        def bank(name):
            return ctx.enter_context(nc.psum_tensor(name, [P, BT], F32))

        def sem(name):
            return ctx.enter_context(nc.semaphore(name))

        wqk_h, wqk_l = sb("wqk_h", [P, C, 2 * D], F32R), sb("wqk_l", [P, C, 2 * D], F32R)
        wvr_h, wvr_l = sb("wvr_h", [P, C, VW], F32R), sb("wvr_l", [P, C, VW], F32R)
        wgu_h, wgu_l = sb("wgu_h", [P, 2, E, C, I], F32R), sb("wgu_l", [P, 2, E, C, I], F32R)
        wd_h, wd_l = sb("wd_h", [P, E, D], F32R), sb("wd_l", [P, E, D], F32R)
        wo_h, wo_l = sb("wo_h", [P, C, D], F32R), sb("wo_l", [P, C, D], F32R)
        conv_ws = sb("conv_ws", [P, C, TAPS])
        conv_bs = sb("conv_bs", [P, C])
        bias_s = sb("bias_s", [P, NR])
        tables_s = sb("tables_s", [P, 3 * P + 2 + T * NR])
        ident_s = tables_s[:, 0:P]
        causal_s = tables_s[:, P:2 * P]
        same_head_s = tables_s[:, 2 * P:3 * P]
        parity_s = tables_s[:, 3 * P:3 * P + 2]
        iota_s = tables_s[:, 3 * P + 2:].rearrange("p (t n) -> p t n", t=T)
        sel = sb("sel", [2 * E, E, P], F32R)
        zeros = sb("zeros", [P, BT])
        half = sb("half", [P, T])
        spare = sb("spare", [P, 1])
        x_t = sb("x_t", [P, 2, T, D])
        xn = sb("xn", [P, T, D])
        stats = sb("stats", [P, T, 6])
        mv = sb("mv", [P, T, 2])
        negm = sb("negm", [P, T])
        vare = sb("vare", [P, T])
        rstd = sb("rstd", [P, T])
        xT = sb("xT", [P, C, HALO + BT])
        xh, xl = sb("xh", [P, C, BT], F32R), sb("xl", [P, C, BT], F32R)
        kT = sb("kT", [P, C, BT])
        kh, kl = sb("kh", [P, C, BT], F32R), sb("kl", [P, C, BT], F32R)
        qT = sb("qT", [P, C, BT])
        qh, ql = sb("qh", [P, C, 2, BT], F32R), sb("ql", [P, C, 2, BT], F32R)
        ksum = sb("ksum", [P, 2, C, BT])
        qks = sb("qks", [P, C, BT])
        den = sb("den", [P, C, BT])
        rden = sb("rden", [P, 2, C, P])
        vp = sb("vp", [P, T, PAIRS, 3, HD])
        score = sb("score", [P, T, NR])
        scoreb = sb("scoreb", [P, T, NR])
        top = sb("top", [P, T, 8])
        topi = sb("topi", [P, T, 8], U32)
        hot = sb("hot", [P, 2, T, NR])
        picked = sb("picked", [P, T, NR])
        wsum = sb("wsum", [P, 3, T])
        cw = sb("cw", [P, T, NR])
        c46 = sb("c46", [P, T, 1])
        cws = sb("cws", [P, T, 2 * E], F32R)
        cwT = sb("cwT", [2 * E, BT], F32R)
        sm = sb("sm", [P, 2, 2 * PAIRS, P])
        ktok = sb("ktok", [P, D])
        state = sb("state", [P, D])
        state_bd = sb("state_bd", [P, D])
        yT = sb("yT", [P, C, BT])
        yh, yl = sb("yh", [P, C, BT], F32R), sb("yl", [P, C, BT], F32R)
        sg = sb("sg", [P, 2, BT])
        gu = sb("gu", [P, BT])
        hid = sb("hid", [P, E, BT])
        hh, hl = sb("hh", [P, E, BT], F32R), sb("hl", [P, E, BT], F32R)
        cT = sb("cT", [P, 2, C, BT])

        same = qks[:, :, :].rearrange("p c n -> p (c n)").rearrange("p (t d) -> p t d", t=T)

        st_qkv = hid[:, :, :].rearrange("p e n -> p (e n)")[:, 0:C * 3 * D].rearrange("p (c n) -> p c n", c=C)
        st_g = sm[:, 0, 0:8, :].rearrange("p h n -> p (h n)").rearrange("p (e c i) -> p e c i", e=E, c=C)
        st_u = sm[:, 0, 8:16, :].rearrange("p h n -> p (h n)").rearrange("p (e c i) -> p e c i", e=E, c=C)
        st_d = yT[:, :, :].rearrange("p c n -> p (c n)").rearrange("p (e n) -> p e n", e=E)
        st_o = ksum[:, 0, 0, :].rearrange("p (c n) -> p c n", c=C)
        st_r = ksum[:, 0, 1, 0:C * NR].rearrange("p (c n) -> p c n", c=C)
        st_sel = ksum[0:2 * E, 1, 0, 0:E * P].rearrange("p (e n) -> p e n", e=E)

        R = [bank(f"ring{k}") for k in range(3)]
        SB = [bank(f"scores{k}") for k in range(2)]
        NUM, TR, ST = bank("num"), bank("turned"), bank("state_add")
        VB = R + [TR]
        KB, QB = [NUM, ST], SB
        GB = [R[0], NUM, R[0], R[0]]
        DB = [R[0], ST]
        XB = [R[0], R[1]]

        tables_in = sem("tables_in")
        qkv_in = sem("qkv_in")
        expert_in = sem("expert_in")
        out_in = sem("out_in")
        small_in = sem("small_in")
        w_split = sem("w_split")
        w_hi = sem("w_hi")
        set_up = sem("set_up")
        x_in = [sem("x_in0"), sem("x_in1")]
        stored = [sem("stored0"), sem("stored1")]
        s_bn = sem("s_bn")
        s_stats = sem("s_stats")
        s_rstd = sem("s_rstd")
        s_xn = sem("s_xn")
        s_xtr = sem("s_xtr")
        s_xT = sem("s_xT")
        s_halo = sem("s_halo")
        s_xh = sem("s_xh")
        s_xl = sem("s_xl")
        s_kp = sem("s_kp")
        s_kT = sem("s_kT")
        s_kh = sem("s_kh")
        s_kl = sem("s_kl")
        s_qp = sem("s_qp")
        s_qT = sem("s_qT")
        s_qh = sem("s_qh")
        s_ql = sem("s_ql")
        s_vp = sem("s_vp")
        s_v = sem("s_v")
        s_sig = sem("s_sig")
        s_cw = sem("s_cw")
        s_cws = sem("s_cws")
        s_cwtr = sem("s_cwtr")
        s_cwT = sem("s_cwT")
        s_qks = sem("s_qks")
        s_denp = sem("s_denp")
        s_den = sem("s_den")
        s_rden = sem("s_rden")
        s_gp = sem("s_gp")
        s_sg = sem("s_sg")
        s_up = sem("s_up")
        s_gu = sem("s_gu")
        s_cwp = sem("s_cwp")
        s_hid = sem("s_hid")
        s_hh = sem("s_hh")
        s_hl = sem("s_hl")
        s_s = sem("s_s")
        s_sm = sem("s_sm")
        s_ktr = sem("s_ktr")
        s_ktok = sem("s_ktok")
        s_num = sem("s_num")
        s_y = sem("s_y")
        s_yh = sem("s_yh")
        s_yl = sem("s_yl")
        s_st = sem("s_st")
        s_state = sem("s_state")
        s_bd = sem("s_bd")
        s_conv = sem("s_conv")
        s_base1 = sem("s_base1")
        s_same = sem("s_same")
        s_relu7 = sem("s_relu7")
        s_base2 = sem("s_base2")
        s_op = sem("s_op")
        s_out = sem("s_out")
        s_own = sem("s_own")

        N_BATCH = n_seq * BPS

        def rounds(engine, body):
            with engine.Fori(0, n_seq - 1) as s:
                for j in range(BPS):
                    body(s, j, BPS)
            for j in range(BPS):
                body(n_seq - 1, j, BPS - 1 - j)

        def at(s, j, per, k):
            return s * (BPS * per) + (j * per + k)

        SPLITS = [(qkv_in, 3, wvr_h[:, :, 0:D], wvr_l[:, :, 0:D], st_qkv[:, :, 2 * D:3 * D])]
        SPLITS += [(qkv_in, 3, wvr_h[:, :, D:VW], wvr_l[:, :, D:VW], st_r)]
        SPLITS += [(qkv_in, 3, wqk_h[:, c, :], wqk_l[:, c, :], st_qkv[:, c, 0:2 * D]) for c in range(C)]
        EARLY = len(SPLITS)
        SPLITS += [(expert_in, 5, wgu_h[:, 0], wgu_l[:, 0], st_g), (expert_in, 5, wgu_h[:, 1], wgu_l[:, 1], st_u)]
        SPLITS += [(out_in, 2, wd_h[:, :, :], wd_l[:, :, :], st_d), (out_in, 2, wo_h[:, :, :], wo_l[:, :, :], st_o)]
        N_SPLITS = len(SPLITS)
        OWN_SETUP = 1 + (TAPS - 1)
        OWN_BATCH = 1 + 11 + 1 + (TAPS - 1)

        def settled(engine):
            engine.wait_ge(set_up, 3)

        block = ctx.enter_context(nc.Block())

        @block.sync
        def _(sp):
            sp.dma_start(x_t[:, 0], x_v[0]).then_inc(x_in[0], 16)
            sp.dma_start(tables_s[:, :], tables).then_inc(tables_in, 16)
            sp.dma_start(st_r, w_router.rearrange("(c p) n -> p c n", p=P)).then_inc(qkv_in, 16)
            for c in range(C):
                sp.dma_start(st_qkv[:, c, :], wqkv[c * P:(c + 1) * P, :]).then_inc(qkv_in, 16)
            sp.dma_start(conv_ws[:, :, :], conv_w).then_inc(small_in, 16)
            sp.dma_start(conv_bs[:, :], conv_b).then_inc(small_in, 16)
            sp.dma_start(bias_s[:, :], router_bias).then_inc(small_in, 16)
            for src, dst in ((w_gate, st_g), (w_up, st_u)):
                for c in range(C):
                    sp.dma_start(dst[:, :, c, :], src[:, c * P:(c + 1) * P, :].rearrange("e p i -> p e i")
                                 ).then_inc(expert_in, 16)
            sp.dma_start(st_sel, expert_rows).then_inc(expert_in, 16)
            sp.dma_start(st_d, w_down.rearrange("e p n -> p e n")).then_inc(out_in, 16)
            sp.dma_start(st_o, wo.rearrange("(c p) n -> p c n", p=P)).then_inc(out_in, 16)
            sp.dma_start(x_t[:, 1], x_v[1]).then_inc(x_in[1], 16)

            def batch(s, j, left):
                b = s * BPS + j
                sp.wait_ge(s_out, at(s, j, T, 2 * T))
                sp.dma_start(out_v[b], x_t[:, j % 2]).then_inc(stored[j % 2], 16)
                if left < 2:
                    return
                sp.wait_ge(stored[j % 2], s * (BPS // 2 * 16) + (j // 2 + 1) * 16)
                sp.dma_start(x_t[:, j % 2], x_v[b + 2]).then_inc(x_in[j % 2], 16)

            rounds(sp, batch)
            for p in range(2):
                sp.wait_ge(stored[p], N_BATCH // 2 * 16)

        @block.tensor
        def _(pe):
            mm = nc.tensor.matmul

            def turn_xn(s, j, k):
                pe.wait_ge(s_xn, at(s, j, 1, k + 1))
                for c in range(C):
                    if k and c == 0:
                        pe.wait_ge(s_sg, at(s, j, T, T))
                    elif k:
                        pe.wait_ge(s_gu, at(s, j, T, T))
                    for t in range(T):
                        ins = nc.tensor.transpose(XB[c][:, t * P:(t + 1) * P], xn[:, t, c * P:(c + 1) * P],
                                                  ident_s[:, :])
                    ins.then_inc(s_xtr, 1)

            def product(dst, pairs, first=True, final=True):
                passes = [q for lh, ll, rh, rl in pairs for q in ((lh, rl), (lh, rh), (ll, rh))]
                for n, (lhs, rhs) in enumerate(passes):
                    ins = mm(dst, lhs, rhs, start=first and n == 0, stop=final and n == len(passes) - 1,
                             skip_group_check=not first)
                return ins

            def batch(s, j, left):
                last = left == 0
                pe.wait_ge(s_xh, at(s, j, C, C))
                pe.wait_ge(s_xl, at(s, j, C, C))

                def project(dst, h, l, col):
                    return product(dst, [(h[:, c, col:col + P], l[:, c, col:col + P], xh[:, c, :], xl[:, c, :])
                                         for c in range(C)])

                for t in range(T):
                    if t < 3:
                        pe.wait_ge(s_out, at(s, j, T, 2 + t))
                    ts = slice(t * P, (t + 1) * P)
                    product(VB[t][:, 0:VW], [(xh[:, c, ts], xl[:, c, ts], wvr_h[:, c, :], wvr_l[:, c, :])
                                                for c in range(C)]).then_inc(s_vp, 1)
                for g in range(C):
                    project(KB[g][:, :], wqk_h, wqk_l, D + g * P).then_inc(s_kp, 1)
                for g in range(C):
                    project(QB[g][:, :], wqk_h, wqk_l, g * P).then_inc(s_qp, 1)

                def scores(t, fs):
                    if t or fs[0]:
                        pe.wait_ge(s_sm, at(s, j, 16, 4 * t + fs[0]))
                    ts = slice(t * P, (t + 1) * P)
                    for g in range(C):
                        for n, (k, q) in enumerate(((kh, ql), (kh, qh), (kl, qh))):
                            for f in fs:
                                rows = slice(32 * f, 32 * f + 32)
                                ins = mm(SB[f % 2][:, g * 2 * P:(g + 1) * 2 * P], k[rows, g, ts], q[rows, g, :, ts],
                                         start=n == 0, stop=n == 2)
                    ins.then_inc(s_s, 1)

                def gate(t, u):
                    product((R[1] if u else GB[t])[:, :], [((wgu_h[:, u, t, c, :]), wgu_l[:, u, t, c, :], xh[:, c, :], xl[:, c, :])
                                         for c in range(C)]).then_inc(s_up if u else s_gp, 1)

                def denominator(g):
                    pe.wait_ge(s_qks, at(s, j, C, g + 1))
                    if g == 0:
                        pe.wait_ge(s_sg, at(s, j, T, 1))
                    mm(DB[g][:, :], same_head_s[:, :], qks[:, g, :], start=True, stop=True).then_inc(s_denp, 1)

                def numerators(t):
                    ts = slice(t * P, (t + 1) * P)
                    if t:
                        pe.wait_ge(s_y, at(s, j, T, t))
                    else:
                        pe.wait_ge(s_sg, at(s, j, T, 2))
                    first_tile = j == 0 and t == 0
                    if not first_tile:
                        pe.wait_ge(s_bd, at(s, j, T, t))
                    if not first_tile:
                        for g in range(C):
                            gs = slice(g * P, (g + 1) * P)
                            mm(NUM[:, gs], state_bd[:, gs], qT[:, g, ts], start=g == 0, stop=False,
                               skip_group_check=True)
                    pe.wait_ge(s_sm, at(s, j, 16, 4 * t + 4))
                    for g in range(C):
                        gs = slice(g * P, (g + 1) * P)
                        for par in range(2):
                            for m in range(PPG):
                                pair = g * PPG + m
                                window = vp[:, t, pair, par:par + 2, :].rearrange("p a d -> p (a d)")
                                ins = mm(NUM[32 * m:32 * m + 32, gs], window, sm[:, t % 2, 2 * pair + par, :],
                                         start=first_tile and par == 0 and g == 0, stop=par == 1,
                                         skip_group_check=True)
                    ins.then_inc(s_num, 1)
                    pe.wait_ge(s_ktok, at(s, j, T, t + 1))
                    if t:
                        pe.wait_ge(s_state, at(s, j, T, t))
                    else:
                        pe.wait_ge(s_den, at(s, j, C, C))
                    for g in range(C):
                        gs = slice(g * P, (g + 1) * P)
                        ins = mm(ST[:, gs], ktok[:, gs], vp[:, t, g * PPG:(g + 1) * PPG, 0:3:2, :],
                                 start=True, stop=True)
                    ins.then_inc(s_st, 1)

                def small(t):
                    if t == 0:
                        pe.wait_ge(s_cwT, at(s, j, 1, 1))
                    else:
                        pe.wait_ge(s_ktok, at(s, j, T, t))
                    ts = slice(t * P, (t + 1) * P)
                    for g in range(C):
                        ins = nc.tensor.transpose(TR[:, g * P:(g + 1) * P], kT[:, g, ts], ident_s[:, :])
                    ins.then_inc(s_ktr, 1)
                    if t == 0:
                        pe.wait_ge(s_sig, at(s, j, T, 3))
                    else:
                        pe.wait_ge(s_hid, at(s, j, T, t))
                    mm(R[2][:, :], sel[:, t, :], cwT[:, :], start=True, stop=True).then_inc(s_cwp, 1)

                pe.wait_ge(w_split, N_SPLITS)
                pe.wait_ge(set_up, 4)
                pe.wait_ge(s_sig, at(s, j, T, 1))
                gate(0, 0)
                pe.wait_ge(s_sig, at(s, j, T, 2))
                gate(0, 1)
                pe.wait_ge(s_kT, at(s, j, C, 1))
                gate(1, 0)
                pe.wait_ge(s_cws, at(s, j, 1, 1))
                for t in range(T):
                    ins = nc.tensor.transpose(TR[0:2 * E, t * P:(t + 1) * P], cws[:, t, :].bitcast(F32), ident_s[:, :])
                ins.then_inc(s_cwtr, 1)
                pe.wait_ge(s_kl, at(s, j, C, C))
                pe.wait_ge(s_ql, at(s, j, C, C))
                for t in range(T):
                    scores(t, (0, 1))
                    if t == 0:
                        small(t)
                        pe.wait_ge(s_gu, at(s, j, T, 1))
                        gate(1, 1)
                    else:
                        numerators(t - 1)
                    if t > 1:
                        pe.wait_ge(s_gu, at(s, j, T, t))
                        gate(t, 1)
                    scores(t, (2, 3))
                    if t > 0:
                        small(t)
                    if t == 0:
                        for g in range(C):
                            denominator(g)
                    elif t < T - 1:
                        if t == 1:
                            pe.wait_ge(s_den, at(s, j, C, 1))
                        else:
                            pe.wait_ge(s_sg, at(s, j, T, t + 1))
                        gate(t + 1, 0)
                    elif not last:
                        turn_xn(s, j, 1)
                numerators(T - 1)

                for t in range(T):
                    ts = slice(t * P, (t + 1) * P)
                    bank_o = R[(t + 2) % 3]
                    if t == 0:
                        pe.wait_ge(s_hid, at(s, j, T, T))
                        pe.wait_ge(s_conv, at(s, j, 1, 1))
                    elif t == 1:
                        if last:
                            pe.wait_ge(s_sg, at(s, j, T, T))
                        else:
                            pe.wait_ge(s_xT, at(s, j, C, C + 1))
                    elif t == 2:
                        if last:
                            pe.wait_ge(s_gu, at(s, j, T, T))
                        else:
                            pe.wait_ge(s_xT, at(s, j, C, 2 * C))
                    else:
                        pe.wait_ge(s_out, at(s, j, T, T + 1))
                    for c in range(C):
                        mm(bank_o[:, c * P:(c + 1) * P], cT[:, j % 2, c, ts], ident_s[:, :], is_transpose=True,
                           start=c == 0, stop=False, skip_group_check=True)
                    pe.wait_ge(s_yh, at(s, j, T, t + 1))
                    pe.wait_ge(s_yl, at(s, j, T, t + 1))
                    product(bank_o[:, 0:D], [(yh[:, c, ts], yl[:, c, ts], wo_h[:, c, :], wo_l[:, c, :])
                                             for c in range(C)], first=False, final=False)
                    for e in range(E):
                        if t == 0:
                            pe.wait_ge(s_hh, at(s, j, T, e + 1))
                            pe.wait_ge(s_hl, at(s, j, T, e + 1))
                        ins = product(bank_o[:, 0:D], [(hh[:, e, ts], hl[:, e, ts], wd_h[:, e, :], wd_l[:, e, :])],
                                      first=False, final=e == E - 1)
                    ins.then_inc(s_op, 1)

            pe.wait_ge(tables_in, 16)
            turn_xn(0, 0, 0)
            pe.wait_ge(w_split, EARLY)
            rounds(pe, batch)

        @block.scalar
        def _(act):
            copy = lambda o, i: nc.scalar.activation(o, i, ACT.Copy)

            def high_weights(splits):
                for loaded, n, hi, _, src in splits:
                    act.wait_ge(loaded, 16 * n)
                    copy(hi, src).then_inc(w_hi, 1)

            def fill_xT(s, j, k):
                if k:
                    act.wait_ge(s_conv, at(s, j, 1, 1))
                if k and j < BPS - 1:
                    act.activation(xT[:, :, 0:HALO], xT[:, :, BT:BT + HALO], ACT.Copy).then_inc(s_halo, 1)
                else:
                    act.activation(xT[:, :, 0:HALO], zeros[:, 0:C * HALO].rearrange("p (c h) -> p c h", c=C),
                                   ACT.Copy).then_inc(s_halo, 1)
                act.wait_ge(s_halo, at(s, j, 1, k + 1))
                for c in range(C):
                    act.wait_ge(s_xtr, at(s, j, C, k * C + c + 1))
                    copy(xT[:, c, HALO:HALO + BT], XB[c][:, :]).then_inc(s_xT, 1)

            def batch(s, j, left):
                last = left == 0
                def silu(t):
                    act.wait_ge(s_gp, at(s, j, T, t + 1))
                    act.activation(sg[:, t % 2, :], GB[t][:, :], ACT.Silu).then_inc(s_sg, 1)

                def high_y(t):
                    act.wait_ge(s_y, at(s, j, T, t + 1))
                    ts = slice(t * P, (t + 1) * P)
                    copy(yh[:, :, ts], yT[:, :, ts]).then_inc(s_yh, 1)

                for t in range(T):
                    act.wait_ge(s_vp, at(s, j, T, t + 1))
                    copy(vp[:, t, :, 0:3:2, :],
                         VB[t][:, 0:D].rearrange("p (a b d) -> p a b d", a=PAIRS, b=2)).then_inc(s_v, 1)
                    act.activation(score[:, t, :], VB[t][:, D:VW], ACT.Sigmoid).then_inc(s_sig, 1)
                for g in range(C):
                    act.wait_ge(s_kp, at(s, j, C, g + 1))
                    act.activation(kT[:, g, :], KB[g][:, :], ACT.Relu).then_inc(s_kT, 1)
                    act.wait_ge(s_kT, at(s, j, C, g + 1))
                    copy(kh[:, g, :], kT[:, g, :]).then_inc(s_kh, 1)
                for g in range(C):
                    act.wait_ge(s_qp, at(s, j, C, g + 1))
                    act.activation(qT[:, g, :], QB[g][:, :], ACT.Relu).then_inc(s_qT, 1)
                    act.wait_ge(s_qT, at(s, j, C, g + 1))
                    for par in range(2):
                        ins = act.activation(qh[:, g, par, :], qT[:, g, :], ACT.Copy, scale=parity_s[:, par:par + 1])
                    ins.then_inc(s_qh, 1)
                for t in range(T):
                    if t != 1:
                        silu(t)
                    if t == 0:
                        silu(1)
                        act.wait_ge(s_cwtr, at(s, j, 1, 1))
                        copy(cwT[:, :], TR[0:2 * E, :]).then_inc(s_cwT, 1)
                    act.wait_ge(s_ktr, at(s, j, T, t + 1))
                    copy(ktok[:, :], TR[:, 0:D]).then_inc(s_ktok, 1)
                    if t == 0:
                        for g in range(C):
                            act.wait_ge(s_denp, at(s, j, C, g + 1))
                            act.activation(den[:, g, :], DB[g][:, :], ACT.Copy, bias=EPS_DEN).then_inc(s_den, 1)
                    if t:
                        high_y(t - 1)
                    act.wait_ge(s_hid, at(s, j, T, t + 1))
                    copy(hh[:, t, :], hid[:, t, :]).then_inc(s_hh, 1)
                    if t == 0:
                        act.wait_ge(s_cw, at(s, j, 1, 1))
                        for tt in range(T):
                            ins = act.activation(same[:, tt, :], xn[:, tt, :], ACT.Copy, scale=c46[:, tt, :])
                        ins.then_inc(s_same, 1)
                    if t == 1:
                        act.wait_ge(s_same, at(s, j, 1, 1))
                        for tt in range(T):
                            ins = act.activation(xn[:, tt, :], xn[:, tt, :], ACT.Relu, scale=cw[:, tt, NR - 1:NR])
                        ins.then_inc(s_relu7, 1)
                if not last:
                    fill_xT(s, j, 1)
                high_y(T - 1)

            high_weights(SPLITS[:EARLY])
            act.wait_ge(set_up, 3)
            fill_xT(0, 0, 0)
            high_weights(SPLITS[EARLY:])
            copy(sel[:, :, :], st_sel).then_inc(set_up, 1)
            act.wait_ge(small_in, 16 * 3)
            act.wait_ge(tables_in, 16)
            rounds(act, batch)

        @block.gpsimd
        def _(pool):
            pool.memset(zeros[:, :], 0.0).then_inc(set_up, 1)
            pool.memset(half[:, :], -0.5).then_inc(set_up, 1)
            pool.memset(vp[:, :, :, :, :], 0.0).then_inc(set_up, 1)

            def normalise(s, j, k):
                pool.wait_ge(s_stats, at(s, j, 1, k + 1))
                pool.tensor_tensor(rstd[:, :], vare[:, :], half[:, :], ALU.pow).then_inc(s_rstd, 1)
                settled(pool)
                pool.wait_ge(s_rstd, at(s, j, 1, k + 1))
                for t in range(T):
                    ins = pool.tensor_scalar(xn[:, t, :], x_t[:, (j + k) % 2, t, :], negm[:, t:t + 1],
                                             rstd[:, t:t + 1], ALU.add, ALU.mult)
                ins.then_inc(s_xn, 1)

            def low_x(s, j, k):
                for c in range(C):
                    pool.wait_ge(s_xh, at(s, j, C, k * C + c + 1))
                    pool.tensor_tensor(xl[:, c, :], xT[:, c, HALO:HALO + BT], xh[:, c, :].bitcast(F32),
                                       ALU.subtract).then_inc(s_xl, 1)

            def batch(s, j, left):
                last = left == 0
                xb = x_t[:, j % 2, :, :]
                for g in range(C):
                    pool.wait_ge(s_kh, at(s, j, C, g + 1))
                    pool.tensor_tensor(kl[:, g, :], kT[:, g, :], kh[:, g, :].bitcast(F32),
                                       ALU.subtract).then_inc(s_kl, 1)
                def keep_blocks(t):
                    pool.wait_ge(s_state, at(s, j, T, t + 1))
                    for g in range(C):
                        gs = slice(g * P, (g + 1) * P)
                        ins = pool.tensor_tensor(state_bd[:, gs], state[:, gs], same_head_s[:, :], ALU.mult)
                    ins.then_inc(s_bd, 1)

                def low_y(t):
                    ts = slice(t * P, (t + 1) * P)
                    pool.wait_ge(s_yh, at(s, j, T, t + 1))
                    pool.tensor_tensor(yl[:, :, ts], yT[:, :, ts], yh[:, :, ts].bitcast(F32),
                                       ALU.subtract).then_inc(s_yl, 1)

                for t in range(T):
                    if t:
                        keep_blocks(t - 1)
                        if t == 2 and not last:
                            pool.wait_ge(s_base2, at(s, j, 1, 1))
                            normalise(s, j, 1)
                        low_y(t - 1)
                    pool.wait_ge(s_hh, at(s, j, T, t + 1))
                    pool.tensor_tensor(hl[:, t, :], hid[:, t, :], hh[:, t, :].bitcast(F32),
                                       ALU.subtract).then_inc(s_hl, 1)
                    if t == 0:
                        pool.wait_ge(s_same, at(s, j, 1, 1))
                        pool.tensor_tensor(xb, xb, same[:, :, :], ALU.add).then_inc(s_base1, 1)
                    if t == 1:
                        pool.wait_ge(s_base1, at(s, j, 1, 1))
                        pool.wait_ge(s_relu7, at(s, j, 1, 1))
                        pool.tensor_tensor(xb, xb, xn[:, :, :], ALU.add).then_inc(s_base2, 1)
                low_y(T - 1)
                if not last:
                    low_x(s, j, 1)
                    keep_blocks(T - 1)

            pool.wait_ge(set_up, 3)
            normalise(0, 0, 0)
            low_x(0, 0, 0)
            pool.wait_ge(tables_in, 16)
            rounds(pool, batch)

        @block.vector
        def _(dve):
            def statistics(s, j, k):
                p = (j + k) % 2
                dve.wait_ge(x_in[p], s * (BPS // 2 * 16) + ((j + k) // 2 + 1) * 16)
                for t in range(T):
                    ins = dve.bn_stats(stats[:, t, :], x_t[:, p, t, :])
                ins.then_inc(s_bn, 1)

            def moments(s, j, k):
                dve.wait_ge(s_bn, at(s, j, 1, k + 1))
                dve.memset(spare[:, :], 0.0)
                for t in range(T):
                    ins = dve.bn_aggr(mv[:, t, :], stats[:, t, :])
                own(ins, s, j)
                dve.tensor_scalar(negm[:, :], mv[:, :, 0], -1.0, None, ALU.mult)
                dve.tensor_scalar(vare[:, :], mv[:, :, 1], EPS_LN, None, ALU.add).then_inc(s_stats, 1)

            count = {"setup": 0, "batch": 0, "in_batch": False}

            def own(ins, s, j, apart=False):
                ins.then_inc(s_own, 1)
                if not count["in_batch"]:
                    count["setup"] += 1
                    dve.wait_ge(s_own, count["setup"])
                    return
                count["batch"] += 1
                dve.wait_ge(s_own, s * (BPS * OWN_BATCH) + (j * OWN_BATCH + count["batch"] + OWN_SETUP))
                if apart:
                    dve.memset(spare[:, :], 0.0)

            def high_x(s, j, k):
                for c in range(C):
                    dve.wait_ge(s_xT, at(s, j, C, k * C + c + 1))
                    dve.tensor_copy(xh[:, c, :], xT[:, c, HALO:HALO + BT]).then_inc(s_xh, 1)

            def router(s, j):
                dve.wait_ge(s_sig, at(s, j, T, T))
                bias_b = bias_s[:, :].unsqueeze(1).to_broadcast([P, T, NR])
                own(dve.tensor_tensor(scoreb[:, :, :], score[:, :, :], bias_b, ALU.add), s, j, apart=True)
                for t in range(T):
                    ins = dve.max(top[:, t, :], scoreb[:, t, :])
                own(ins, s, j, apart=True)
                for t in range(T):
                    ins = dve.max_index(topi[:, t, :], top[:, t, :], scoreb[:, t, :])
                own(ins, s, j)
                for n in range(2):
                    ins = dve.tensor_tensor(hot[:, n, :, :], iota_s[:, :, :],
                                            topi[:, :, n:n + 1].to_broadcast([P, T, NR]), ALU.is_equal)
                own(ins, s, j)
                own(dve.tensor_tensor(hot[:, 0, :, :], hot[:, 0, :, :], hot[:, 1, :, :], ALU.add), s, j)
                own(dve.tensor_tensor(picked[:, :, :], hot[:, 0, :, :], score[:, :, :], ALU.mult), s, j)
                own(dve.tensor_reduce(wsum[:, 0, :], picked[:, :, :], AX.X, ALU.add), s, j)
                own(dve.tensor_scalar(wsum[:, 1, :], wsum[:, 0, :], EPS_W, None, ALU.add), s, j)
                own(dve.reciprocal(wsum[:, 2, :], wsum[:, 1, :]), s, j)
                own(dve.tensor_tensor(cw[:, :, :], picked[:, :, :],
                                      wsum[:, 2, :].unsqueeze(2).to_broadcast([P, T, NR]), ALU.mult), s, j)
                own(dve.tensor_copy(cws[:, :, 0:E], cw[:, :, 0:E]), s, j)
                dve.tensor_tensor(cws[:, :, E:2 * E], cw[:, :, 0:E], cws[:, :, 0:E].bitcast(F32),
                                  ALU.subtract).then_inc(s_cws, 1)
                dve.tensor_tensor(c46[:, :, :], cw[:, :, E:E + 1], cw[:, :, E + 2:E + 3], ALU.add).then_inc(s_cw, 1)

            def conv_tap(s, j, k, tap):
                for c in range(C):
                    src, dst = xT[:, c, tap:tap + BT], cT[:, (j + k) % 2, c, :]
                    if tap == 0:
                        ins = dve.tensor_scalar(dst, src, conv_ws[:, c, 0:1], conv_bs[:, c:c + 1], ALU.mult, ALU.add)
                    else:
                        ins = dve.scalar_tensor_tensor(out=dst, in0=src, scalar=conv_ws[:, c, tap:tap + 1],
                                                       in1=dst, op0=ALU.mult, op1=ALU.add)
                if tap < TAPS - 1:
                    own(ins, s, j)
                else:
                    ins.then_inc(s_conv, 1)

            def batch(s, j, left):
                last = left == 0
                count["batch"], count["in_batch"] = 0, True
                router(s, j)
                for g in range(C):
                    dve.wait_ge(s_kT, at(s, j, C, g + 1))
                    before = ksum[:, (j + 1) % 2, g, BT - 1:BT] if j else 0.0
                    ins = dve.tensor_tensor_scan(ksum[:, j % 2, g, :], kT[:, g, :], zeros[:, :], before,
                                                 ALU.add, ALU.add)
                own(ins, s, j)
                for g in range(C):
                    dve.wait_ge(s_qh, at(s, j, C, g + 1))
                    for par in range(2):
                        ins = dve.scalar_tensor_tensor(out=ql[:, g, par, :], in0=qT[:, g, :],
                                                       scalar=parity_s[:, par:par + 1],
                                                       in1=qh[:, g, par, :].bitcast(F32),
                                                       op0=ALU.mult, op1=ALU.subtract)
                    ins.then_inc(s_ql, 1)
                for g in range(C):
                    dve.tensor_tensor(qks[:, g, :], qT[:, g, :], ksum[:, j % 2, g, :], ALU.mult).then_inc(s_qks, 1)

                def mask(t, f):
                    dve.wait_ge(s_s, at(s, j, 8, 2 * t + f // 2 + 1))
                    heads = sm[:, t % 2, :, :].rearrange("p (g m a) n -> p g m (a n)", g=C, a=2)[:, :, f, :]
                    dve.tensor_tensor(heads.rearrange("p g (a n) -> p g a n", a=2),
                                      SB[f % 2][:, :].rearrange("p (g a n) -> p g a n", g=C, a=2),
                                      causal_s[:, :].unsqueeze(1).unsqueeze(1).to_broadcast([P, C, 2, P]),
                                      ALU.mult).then_inc(s_sm, 1)

                def gate_up(t):
                    dve.wait_ge(s_sg, at(s, j, T, t + 1))
                    dve.wait_ge(s_up, at(s, j, T, t + 1))
                    dve.tensor_tensor(gu[:, :], R[1][:, :], sg[:, t % 2, :], ALU.mult).then_inc(s_gu, 1)

                def invert(t):
                    if t == 0:
                        dve.wait_ge(s_den, at(s, j, C, C))
                    dve.reciprocal(rden[:, t % 2], den[:, :, t * P:(t + 1) * P]).then_inc(s_rden, 1)

                def attend(t):
                    ts = slice(t * P, (t + 1) * P)
                    dve.wait_ge(s_rden, at(s, j, T, t + 1))
                    dve.wait_ge(s_num, at(s, j, T, t + 1))
                    dve.tensor_tensor(yT[:, :, ts], NUM[:, 0:D].rearrange("p (g n) -> p g n", g=C), rden[:, t % 2],
                                      ALU.mult).then_inc(s_y, 1)
                    dve.wait_ge(s_st, at(s, j, T, t + 1))
                    if j == 0 and t == 0:
                        dve.tensor_copy(state[:, :], ST[:, 0:D]).then_inc(s_state, 1)
                    else:
                        dve.tensor_tensor(state[:, :], ST[:, 0:D], state[:, :], ALU.add).then_inc(s_state, 1)

                gate_up(0)
                for t in range(T):
                    mask(t, 0)
                    mask(t, 1)
                    if t == 0 and not last:
                        statistics(s, j, 1)
                    if t > 0:
                        if t > 1:
                            invert(t - 1)
                        attend(t - 1)
                        gate_up(t)
                    mask(t, 2)
                    mask(t, 3)
                    dve.wait_ge(s_gu, at(s, j, T, t + 1))
                    dve.wait_ge(s_cwp, at(s, j, T, t + 1))
                    dve.tensor_tensor(hid[:, t, :], R[2][:, :], gu[:, :], ALU.mult).then_inc(s_hid, 1)
                    if t == 0:
                        if not last:
                            moments(s, j, 1)
                        invert(t)
                invert(T - 1)
                attend(T - 1)
                if not last:
                    high_x(s, j, 1)
                dve.wait_ge(s_base2, at(s, j, 1, 1))
                for t in range(T):
                    dve.wait_ge(s_op, at(s, j, T, t + 1))
                    xb = x_t[:, j % 2, t, :]
                    dve.tensor_tensor(xb, R[(t + 2) % 3][:, 0:D], xb, ALU.add).then_inc(s_out, 1)
                    if not last:
                        conv_tap(s, j, 1, t)
                if not last:
                    assert count["batch"] == OWN_BATCH, count

            def low_weights(first, stop):
                for n in range(first, stop):
                    _, _, hi, lo, src = SPLITS[n]
                    dve.wait_ge(w_hi, n + 1)
                    dve.tensor_tensor(lo, src, hi.bitcast(F32), ALU.subtract).then_inc(w_split, 1)

            statistics(0, 0, 0)
            moments(0, 0, 0)
            for n in range(T):
                dve.memset(gu[:, n:n + 1], 0.0).then_inc(s_out, 1)
            low_weights(0, EARLY)
            high_x(0, 0, 0)
            low_weights(EARLY, N_SPLITS)
            dve.wait_ge(small_in, 16 * 3)
            dve.wait_ge(tables_in, 16)
            dve.wait_ge(set_up, 4)
            for tap in range(TAPS):
                conv_tap(0, 0, 0, tap)
            rounds(dve, batch)


_INS = ["L0_attn_x", "L0_attn_wqkv", "L0_attn_wo", "L0_ffn_Wr", "L0_ffn_router_bias", "L0_ffn_Wg", "L0_ffn_Wu",
        "L0_ffn_Wd", "L0_ffn_conv_w", "L0_ffn_conv_b"]


def _constants():
    import numpy as np
    f = np.float32
    p = np.arange(128)
    ident = (p[:, None] == p[None, :]).astype(f)
    causal = (p[:, None] <= p[None, :]).astype(f)
    same_head = (p[:, None] // 16 == p[None, :] // 16).astype(f)
    parity = np.stack([(p // 16) % 2 == 0, (p // 16) % 2 == 1], 1).astype(f)
    rows = np.zeros((8, 4, 128), f)
    for e in range(4):
        rows[e, e] = rows[4 + e, e] = 1.0
    iota = np.broadcast_to(np.tile(np.arange(8, dtype=f), 4), (128, 32))
    return {"tables": np.concatenate([ident, causal, same_head, parity, iota], 1), "expert_rows": rows}


def kernel(**inputs):
    import numpy as _np
    import concourse.bacc as _bacc
    from concourse import mybir as _mybir
    from concourse.bass_utils import run_bass_kernel_spmd as _run

    nc = _bacc.Bacc("TRN2", target_bir_lowering=False, num_devices=1)
    arrays, args = {}, []
    given = {name: inputs[name] for name in _INS}
    given["L0_ffn_conv_w"] = _np.asarray(given["L0_ffn_conv_w"])[:, 0, :].T.reshape(2, 128, 4).transpose(1, 0, 2)
    given["L0_ffn_conv_b"] = _np.asarray(given["L0_ffn_conv_b"]).reshape(2, 128).T
    given["L0_ffn_router_bias"] = _np.broadcast_to(_np.asarray(given["L0_ffn_router_bias"]), (128, 8))
    given.update(_constants())
    for name, a in given.items():
        a = _np.ascontiguousarray(a)
        arrays[f"in_{name}_dram"] = a
        args.append(nc.dram_tensor(f"in_{name}_dram", a.shape, _mybir.dt.from_np(a.dtype), kind="ExternalInput").ap())
    shape = tuple(inputs["L0_attn_x"].shape)
    args.append(nc.dram_tensor("out_0_dram", shape, _mybir.dt.float32, kind="ExternalOutput").ap())
    layer_kernel(nc, *args)
    r = _run(nc, [arrays], core_ids=[0])
    return r.results[0]["out_0_dram"]
```
